# Optimizing a Trainium2 kernel written in Bass

```python
import numpy as np
import jax
import jax.numpy as jnp

def _softmax(x, axis=-1):
    return jax.nn.softmax(x, axis=axis)

def _gelu(x):
    return jax.nn.gelu(x, approximate=True)

def _silu(x):
    return jax.nn.silu(x)

def _sigmoid(x):
    return jax.nn.sigmoid(x)

def _layernorm(x, axis=-1, eps=1e-05):
    m = jnp.mean(x, axis=axis, keepdims=True)
    v = jnp.var(x, axis=axis, keepdims=True)
    return (x - m) / jnp.sqrt(v + eps)

def _scatter_add(tgt, idx, src, axis=0):
    return tgt.at[idx].add(src)

def _segment_sum(src, seg, n):
    return jax.ops.segment_sum(src, seg, n)
kernel_name = 'mk_gnn_resnorm_d2_gnn_r8_cd8d7b'

def setup_inputs(seed: int=0):
    np.random.seed(seed)
    _w = jnp.asarray

    def _rec_inputs():
        import jax
        import jax.numpy as jnp
        _gk = jax.random.key(seed)
        x = -0.0003019 + 1 * jax.random.normal(jax.random.fold_in(_gk, 1), (1250, 1024), jnp.float32)
        src = jax.random.randint(jax.random.fold_in(_gk, 2), (40000,), 0, 1250, jnp.int32)
        dst = jax.random.randint(jax.random.fold_in(_gk, 3), (40000,), 0, 1250, jnp.int32)
        _o = jnp.argsort(dst, stable=True)
        src = src[_o]
        dst = dst[_o]
        edge_type_2 = jax.random.randint(jax.random.fold_in(_gk, 12), (40000,), 0, 2, jnp.int32)
        return (x, src, dst, edge_type_2)
    x, src, dst, edge_type_2 = _rec_inputs()

    def _L0_gnn_setup():
        import jax, jax.numpy as jnp
        import numpy as np
        D_MODEL = 1024
        D_FF = 286
        NUM_REL = 2
        EPS = 1e-06

        def t5_layer_norm(x, weight):
            var = jnp.mean(jnp.square(x.astype(jnp.float32)), axis=-1, keepdims=True)
            return weight * (x * jax.lax.rsqrt(var + EPS))

        def rgcn_conv(x, edge_index, edge_type, W_rel, W_root, bias):
            N = x.shape[0]
            src, dst = (edge_index[0], edge_index[1])
            h_src = x[src]
            out = x @ W_root + bias
            for r in range(NUM_REL):
                w = (edge_type == r).astype(x.dtype)
                msg = h_src @ W_rel[r] * w[:, None]
                sums = jax.ops.segment_sum(msg, dst, num_segments=N)
                cnt = jax.ops.segment_sum(w, dst, num_segments=N)
                out = out + sums / jnp.maximum(cnt, 1.0)[:, None]
            return out
        key = jax.random.key(seed)
        ks = jax.random.split(key, 8)
        N, E = (2500, 40000)
        hidden_states = jax.random.normal(ks[0], (N, D_MODEL), dtype=jnp.float32)
        edge_index = jax.random.randint(ks[1], (2, E), 0, N, dtype=jnp.int64)
        edge_type = jax.random.randint(ks[2], (E,), 0, NUM_REL, dtype=jnp.int64)
        ln_weight = jnp.ones((D_MODEL,), dtype=jnp.float32)
        W_rel = jax.random.normal(ks[3], (NUM_REL, D_MODEL, D_FF), dtype=jnp.float32) * (1.0 / np.sqrt(D_MODEL))
        W_root = jax.random.normal(ks[4], (D_MODEL, D_FF), dtype=jnp.float32) * (1.0 / np.sqrt(D_MODEL))
        conv_bias = jnp.zeros((D_FF,), dtype=jnp.float32)
        wo_weight = jax.random.normal(ks[5], (D_FF, D_MODEL), dtype=jnp.float32) * (1.0 / np.sqrt(D_FF))
        return {'hidden_states': hidden_states, 'edge_index': edge_index, 'edge_type': edge_type, 'ln_weight': ln_weight, 'W_rel': W_rel, 'W_root': W_root, 'conv_bias': conv_bias, 'wo_weight': wo_weight}
    _L0_gnn_all = _L0_gnn_setup()
    _L0_gnn_in = {k: v for k, v in _L0_gnn_all.items() if k in ('ln_weight', 'W_rel', 'W_root', 'conv_bias', 'wo_weight')}
    del _L0_gnn_all

    def _L1_gnn_setup():
        import jax, jax.numpy as jnp
        import numpy as np
        N = 6250
        E = 100000
        D_IN = 1024
        D_HID = 512
        D_B = 256
        N_LAYERS = 3
        LN_EPS = 1e-05

        def layernorm(x, g, b):
            m = jnp.mean(x, axis=-1, keepdims=True)
            v = jnp.mean((x - m) ** 2, axis=-1, keepdims=True)
            return (x - m) * jax.lax.rsqrt(v + LN_EPS) * g + b
        key = jax.random.key(seed)
        ks = jax.random.split(key, 16)
        s = 0.02
        inp = {'x': jax.random.normal(ks[0], (N, D_IN), dtype=jnp.float32), 'edge_index': jax.random.randint(ks[1], (2, E), 0, N, dtype=jnp.int32), 'ln_in_g': jnp.ones((D_IN,), jnp.float32), 'ln_in_b': jnp.zeros((D_IN,), jnp.float32), 'W1': jax.random.normal(ks[2], (D_IN, D_HID), jnp.float32) * s, 'b1': jnp.zeros((D_HID,), jnp.float32), 'W2': jax.random.normal(ks[3], (D_HID, D_B), jnp.float32) * s, 'b2': jnp.zeros((D_B,), jnp.float32), 'layer_Wa': jax.random.normal(ks[4], (N_LAYERS, D_B, D_B), jnp.float32) * s, 'layer_ba': jnp.zeros((N_LAYERS, D_B), jnp.float32), 'layer_Wb': jax.random.normal(ks[5], (N_LAYERS, D_B, D_B), jnp.float32) * s, 'layer_bb': jnp.zeros((N_LAYERS, D_B), jnp.float32), 'layer_ng': jnp.ones((N_LAYERS, D_B), jnp.float32), 'layer_nb': jnp.zeros((N_LAYERS, D_B), jnp.float32), 'Wd1': jax.random.normal(ks[6], (D_B, D_HID), jnp.float32) * s, 'bd1': jnp.zeros((D_HID,), jnp.float32), 'Wd2': jax.random.normal(ks[7], (D_HID, D_IN), jnp.float32) * s, 'bd2': jnp.zeros((D_IN,), jnp.float32), 'out_g': jnp.ones((D_IN,), jnp.float32), 'out_b': jnp.zeros((D_IN,), jnp.float32)}
        return inp
    _L1_gnn_all = _L1_gnn_setup()
    _L1_gnn_in = {k: v for k, v in _L1_gnn_all.items() if k in ('ln_in_g', 'ln_in_b', 'W1', 'b1', 'W2', 'b2', 'layer_Wa', 'layer_ba', 'layer_Wb', 'layer_bb', 'layer_ng', 'layer_nb', 'Wd1', 'bd1', 'Wd2', 'bd2', 'out_g', 'out_b')}
    del _L1_gnn_all
    return {'x': x, 'src': src, 'dst': dst, 'edge_type_2': edge_type_2, 'L0_gnn_ln_weight': _L0_gnn_in['ln_weight'], 'L0_gnn_W_rel': _L0_gnn_in['W_rel'], 'L0_gnn_W_root': _L0_gnn_in['W_root'], 'L0_gnn_conv_bias': _L0_gnn_in['conv_bias'], 'L0_gnn_wo_weight': _L0_gnn_in['wo_weight'], 'L1_gnn_ln_in_g': _L1_gnn_in['ln_in_g'], 'L1_gnn_ln_in_b': _L1_gnn_in['ln_in_b'], 'L1_gnn_W1': _L1_gnn_in['W1'], 'L1_gnn_b1': _L1_gnn_in['b1'], 'L1_gnn_W2': _L1_gnn_in['W2'], 'L1_gnn_b2': _L1_gnn_in['b2'], 'L1_gnn_layer_Wa': _L1_gnn_in['layer_Wa'], 'L1_gnn_layer_ba': _L1_gnn_in['layer_ba'], 'L1_gnn_layer_Wb': _L1_gnn_in['layer_Wb'], 'L1_gnn_layer_bb': _L1_gnn_in['layer_bb'], 'L1_gnn_layer_ng': _L1_gnn_in['layer_ng'], 'L1_gnn_layer_nb': _L1_gnn_in['layer_nb'], 'L1_gnn_Wd1': _L1_gnn_in['Wd1'], 'L1_gnn_bd1': _L1_gnn_in['bd1'], 'L1_gnn_Wd2': _L1_gnn_in['Wd2'], 'L1_gnn_bd2': _L1_gnn_in['bd2'], 'L1_gnn_out_g': _L1_gnn_in['out_g'], 'L1_gnn_out_b': _L1_gnn_in['out_b']}

def reference(x, src, dst, edge_type_2, L0_gnn_ln_weight, L0_gnn_W_rel, L0_gnn_W_root, L0_gnn_conv_bias, L0_gnn_wo_weight, L1_gnn_ln_in_g, L1_gnn_ln_in_b, L1_gnn_W1, L1_gnn_b1, L1_gnn_W2, L1_gnn_b2, L1_gnn_layer_Wa, L1_gnn_layer_ba, L1_gnn_layer_Wb, L1_gnn_layer_bb, L1_gnn_layer_ng, L1_gnn_layer_nb, L1_gnn_Wd1, L1_gnn_bd1, L1_gnn_Wd2, L1_gnn_bd2, L1_gnn_out_g, L1_gnn_out_b):
    import jax
    import jax.numpy as jnp

    def _L0_gnn_ref(hidden_states, edge_index, edge_type, ln_weight, W_rel, W_root, conv_bias, wo_weight):
        import jax, jax.numpy as jnp
        import numpy as np
        D_MODEL = 1024
        D_FF = 286
        NUM_REL = 2
        EPS = 1e-06

        def t5_layer_norm(x, weight):
            var = jnp.mean(jnp.square(x.astype(jnp.float32)), axis=-1, keepdims=True)
            return weight * (x * jax.lax.rsqrt(var + EPS))

        def rgcn_conv(x, edge_index, edge_type, W_rel, W_root, bias):
            N = x.shape[0]
            src, dst = (edge_index[0], edge_index[1])
            h_src = x[src]
            out = x @ W_root + bias
            for r in range(NUM_REL):
                w = (edge_type == r).astype(x.dtype)
                msg = h_src @ W_rel[r] * w[:, None]
                sums = jax.ops.segment_sum(msg, dst, num_segments=N)
                cnt = jax.ops.segment_sum(w, dst, num_segments=N)
                out = out + sums / jnp.maximum(cnt, 1.0)[:, None]
            return out
        norm_x = t5_layer_norm(hidden_states, ln_weight)
        y = jax.nn.elu(rgcn_conv(norm_x, edge_index, edge_type, W_rel, W_root, conv_bias))
        y = y @ wo_weight
        return hidden_states + y

    def _L1_gnn_ref(x, edge_index, ln_in_g, ln_in_b, W1, b1, W2, b2, layer_Wa, layer_ba, layer_Wb, layer_bb, layer_ng, layer_nb, Wd1, bd1, Wd2, bd2, out_g, out_b):
        import jax, jax.numpy as jnp
        import numpy as np
        N = 6250
        E = 100000
        D_IN = 1024
        D_HID = 512
        D_B = 256
        N_LAYERS = 3
        LN_EPS = 1e-05

        def layernorm(x, g, b):
            m = jnp.mean(x, axis=-1, keepdims=True)
            v = jnp.mean((x - m) ** 2, axis=-1, keepdims=True)
            return (x - m) * jax.lax.rsqrt(v + LN_EPS) * g + b
        n = x.shape[0]
        src, dst = (edge_index[0], edge_index[1])
        h = layernorm(x, ln_in_g, ln_in_b)
        h = jax.nn.relu(h @ W1 + b1)
        h = h @ W2 + b2
        for i in range(N_LAYERS):
            agg = jax.ops.segment_sum(h[src], dst, num_segments=n)
            z = h + agg
            z = jax.nn.relu(z @ layer_Wa[i] + layer_ba[i])
            z = z @ layer_Wb[i] + layer_bb[i]
            z = jax.nn.relu(layernorm(z, layer_ng[i], layer_nb[i]))
            h = h + z
        delta = jax.nn.relu(h @ Wd1 + bd1) @ Wd2 + bd2
        return layernorm(x + delta, out_g, out_b)
    edge_index = jnp.stack([src, dst])
    x = _layernorm(x + _L0_gnn_ref(x, edge_index, edge_type_2, L0_gnn_ln_weight, L0_gnn_W_rel, L0_gnn_W_root, L0_gnn_conv_bias, L0_gnn_wo_weight), axis=-1)
    x = _layernorm(x + _L1_gnn_ref(x, edge_index, L1_gnn_ln_in_g, L1_gnn_ln_in_b, L1_gnn_W1, L1_gnn_b1, L1_gnn_W2, L1_gnn_b2, L1_gnn_layer_Wa, L1_gnn_layer_ba, L1_gnn_layer_Wb, L1_gnn_layer_bb, L1_gnn_layer_ng, L1_gnn_layer_nb, L1_gnn_Wd1, L1_gnn_bd1, L1_gnn_Wd2, L1_gnn_bd2, L1_gnn_out_g, L1_gnn_out_b), axis=-1)
    return x

_drawn_inputs = setup_inputs


def setup_inputs(seed=0):
    import zlib

    import numpy as np

    out = dict(_drawn_inputs(seed))
    spreads = {'L0_gnn_ln_weight': (1.0, 0.2),
     'L0_gnn_conv_bias': (0.0, 0.1),
     'L1_gnn_ln_in_g': (1.0, 0.6),
     'L1_gnn_ln_in_b': (0.0, 0.8),
     'L1_gnn_b1': (0.0, 2.0),
     'L1_gnn_b2': (0.0, 1.102),
     'L1_gnn_layer_ba': (0.0, 2.0),
     'L1_gnn_layer_bb': (0.0, 2.0),
     'L1_gnn_layer_ng': (1.0, 0.6),
     'L1_gnn_layer_nb': (0.0, 0.8),
     'L1_gnn_bd1': (0.0, 0.472),
     'L1_gnn_bd2': (0.0, 0.1),
     'L1_gnn_out_g': (1.0, 0.2),
     'L1_gnn_out_b': (0.0, 0.1)}
    factors = {'L1_gnn_W1': 5.138}
    for name, (base, spread) in spreads.items():
        noise = np.random.default_rng([zlib.crc32(name.encode()), seed]).standard_normal(out[name].shape)
        drawn = base * np.exp(spread * noise) if base else spread * noise
        out[name] = jnp.asarray(drawn.astype(out[name].dtype))
    for name, factor in factors.items():
        out[name] = (out[name] * factor).astype(out[name].dtype)
    return out
```

```python
from contextlib import ExitStack

import concourse.bass as bass
from concourse import mybir

ALU = mybir.AluOpType
ACT = mybir.ActivationFunctionType
AX = mybir.AxisListType
F32 = mybir.dt.float32
F16 = mybir.dt.float16
BF16 = mybir.dt.bfloat16
I32 = mybir.dt.int32

N, D, E = 1250, 1024, 40000
P = 125
T = N // P
KD = D // 128
R, F = 2, 286
FW = 3 * F
FB = [128, 128, F - 256]
J = 4
G = E // (P * J)
GP = G + 4
W = 32
NW = -(-N // W)
C = T * W
ND = N + W
H1, HB, L = 512, 256, 3
K1, K2 = H1 // 128, HB // 128
FAR = 4096
UG = G // T
CH = [(0, 500), (500, 500), (1000, 250)]
EPS0, EPS = 1e-6, 1e-5


def graph_kernel(nc, x, src, dst, typ, ln_w, w_rel, w_root, conv_b, wo, g_in, b_in, w1, b1, w2, b2,
                 wa, ba, wb, bb, ng, nb, wd1, bd1, wd2, bd2, g_out, b_out, out):
    with ExitStack() as ctx:
        top = [16512]

        def at(off, name, shape, dt):
            return nc.alloc_sbuf_tensor_at(name, shape, dt, offset=off)

        def size(shape, dt):
            n = 2 if dt in (F16, BF16) else 4
            for k in shape[1:]:
                n *= k
            return -(-n // 32) * 32

        def stack(base, items):
            got = []
            for name, shape, dt in items:
                got.append(at(base, name, shape, dt))
                base += size(shape, dt)
            return got, base

        (adj, ident, eps0, epsc, ones, xt, seln, zero, rc), base = stack(top[0], [
            ("adj", [P, R, T, ND], F32), ("ident", [128, 128], F32), ("eps0", [P, 1], F32),
            ("epsc", [P, 1], F32), ("ones", [P, 1], F32), ("xt", [P, D], F32), ("seln", [1, 2], I32), ("zero", [P, 1], F32), ("rc", [P, 2, 2], F32)])
        y_base = base
        (y,), base = stack(base, [("y", [P, T, FW + 2], F32)])
        rows = [(n, [G, J * P], d) for n, d in (
            ("src_i", I32), ("dst_i", I32), ("typ_i", I32), ("e_low", F32), ("e_code", F32),
            ("e_base", F32), ("e_far", F32), ("e_rel", F32))]
        (src_i, dst_i, typ_i, e_low, e_code, e_base, e_far, e_rel, e_blk, gmin), end = stack(
            y_base, rows + [("e_blk", [G, J * P], F32), ("gmin", [G, 2], F32)])
        assert end <= base
        p1 = base
        (w_all, xn, xnT, oh_low, oh_code, iota_c, iota_l, iota_r, iota_i, edgeT, codeS, maskS, lnw,
         mini, small1), end1 = stack(p1, [
             ("w_all", [128, KD, FW], F32), ("xn", [P, D], F32), ("xnT", [128, KD, P], F32),
             ("oh_low", [P, 2, J, P], BF16), ("oh_code", [P, 2, J, R * C], BF16),
             ("iota_c", [P, R * C], F16), ("iota_l", [P, P], F16), ("iota_r", [128, 128], F32),
             ("iota_i", [128, 1], F32), ("edgeT", [P, 4, J, GP], F32), ("codeS", [P, J, GP], F32),
             ("maskS", [P, 2, J, GP], F32), ("lnw", [128, KD], F32), ("mini", [1, GP], I32),
             ("small1", [P, 8], F32)])
        (x1, wo_s, cb_b, ybuf, yT, mv, small2, st2), end2 = stack(p1, [
            ("x1", [P, T, D], F32), ("wo_s", [128, 3, D], F32), ("cb_b", [P, F], F32),
            ("ybuf", [P, 5, F], F32), ("yT", [128, 3, P], F32), ("mv", [P, T, 2], F32),
            ("small2", [P, 2, T + 2], F32), ("st2", [P, 2, 6], F32)])
        adj1 = top[0] + size([P, T, ND], F32)
        adj1_end = top[0] + size([P, R, T, ND], F32)
        (w1_s, w2_s, xh, hT, r1T, zT), end3 = stack(adj1, [
            ("w1_s", [128, KD, H1], F32), ("w2_s", [128, K1, HB], F32), ("xh", [P, 2, D], F32),
            ("hT", [128, KD, 2 * P], F32), ("r1T", [128, K1, 2 * P], F32), ("zT", [128, K2, N], F32)])
        assert end3 <= adj1_end, (end3, adj1_end)
        (wd1_s, wd2_s, dT, h3T), end5 = stack(adj1, [
            ("wd1_s", [128, K2, H1], F32), ("wd2_s", [128, K1, D], F32),
            ("dT", [128, K1, 2 * P], F32), ("h3T", [128, K2, 2 * P], F32)])
        (h, wa_s, wb_s, rT, bb_b, ng_b, nb_b), end4 = stack(y_base, [
            ("h", [P, T, HB], F32), ("wa_s", [128, K2, HB], F32), ("wb_s", [128, K2, HB], F32),
            ("rT", [128, K2, N], F32), ("bb_b", [P, L, HB], F32), ("ng_b", [P, L, HB], F32),
            ("nb_b", [P, L, HB], F32)])
        (b2_b, g_c, b_c, b1_c, ba_c, bd1_c, zt, st4, small4, mv4), end4b = stack(max(end1, end2), [
            ("b2_b", [P, HB], F32), ("g_c", [128, KD], F32), ("b_c", [128, KD], F32),
            ("b1_c", [128, K1], F32), ("ba_c", [128, K2], F32), ("bd1_c", [128, K1], F32),
            ("zt", [P, 4, HB], F32), ("st4", [P, 2, 6], F32), ("small4", [P, 8], F32), ("mv4", [P, 2, 2], F32)])
        assert end4 <= p1, (end4, p1)
        assert end4b <= nc.sbuf_usable_end, (end1, end2, end4b)
        (bd2_b, go_b, bo_b, ot), end5b = stack(p1 + size([P, T, D], F32), [
            ("bd2_b", [P, D], F32), ("go_b", [P, D], F32), ("bo_b", [P, D], F32), ("ot", [P, D], F32)])
        (ot2, ot3), end5c = stack(end5, [("ot2", [P, D], F32), ("ot3", [P, D], F32)])
        assert end5b <= end4b - size([P, HB], F32)

        pb = ctx.enter_context(nc.psum_tensor("banks", [128, 8, 512], F32))

        def sem(name):
            return ctx.enter_context(nc.semaphore(name))

        def tiled(a):
            return a.rearrange("(t p) d -> t p d", p=P)

        def column(a):
            return a.rearrange("(k p) -> p k", p=128)

        def spread(a):
            return a.rearrange("(o d) -> o d", o=1).broadcast_to([P, a.shape[0]])

        x_t, out_t = tiled(x), tiled(out)

        consts_in, edges_in, x_in, w_in = sem("consts_in"), sem("edges_in"), sem("x_in"), sem("w_in")
        wo_in, w12_in, wab_in, wd_in, rows_in = (sem("wo_in"), sem("w12_in"), sem("wab_in"),
                                                 sem("wd_in"), sem("rows_in"))
        iotas, adj_zero, small_set = sem("iotas"), sem("adj_zero"), sem("small_set")
        prep, edges_ready, edges_ps, codes_ready = (sem("prep"), sem("edges_ready"), sem("edges_ps"),
                                                    sem("codes_ready"))
        onehots, counts_mm, counts_free = sem("onehots"), sem("counts_mm"), sem("counts_free")
        xn_sq, xn_sd, xn_rstd, xn_ready = sem("xn_sq"), sem("xn_sd"), sem("xn_rstd"), sem("xn_ready")
        xnT_ps, xnT_copied, proj_mm, y_copied = (sem("xnT_ps"), sem("xnT_copied"), sem("proj_mm"),
                                                 sem("y_copied"))
        s_codes, s_onehots, s_counts_mm, s_added = (sem("s_codes"), sem("s_onehots"),
                                                    sem("s_counts_mm"), sem("s_added"))
        adj_done = sem("adj_done")
        agg_mm, root_b, cnt_max, cnt_rcp, rel0_added, pre_elu, neg_part, elu_parts, elu_done = (
            sem(n) for n in ("agg_mm", "root_b", "cnt_max", "cnt_rcp", "rel0_added", "pre_elu",
                             "neg_part", "elu_parts", "elu_done"))
        adj_sum, adj_self, yT_ps, yT_copied, wo_mm, res_done, res_stats, res_mv = (
            sem(n) for n in ("adj_sum", "adj_self", "yT_ps", "yT_copied", "wo_mm", "res_done",
                             "res_stats", "res_mv"))
        ln1_sd, ln1_rstd, ln1_shift, x1_ready, x1_stats, x1_mv, ln2_sd, ln2_rstd, ln2_shift = (
            sem(n) for n in ("ln1_sd", "ln1_rstd", "ln1_shift", "x1_ready", "x1_stats", "x1_mv",
                             "ln2_sd", "ln2_rstd", "ln2_shift"))
        xh_ready, xhT_ps, hT_lo, hT_hi, r1_mm, r1_done, h_mm, h_done = (
            sem(n) for n in ("xh_ready", "xhT_ps", "hT_lo", "hT_hi", "r1_mm", "r1_done", "h_mm",
                             "h_done"))
        z_mm, z_lo, z_hi, wa_mm, r_lo, r_hi, wb_mm, z_b, z_stats, z_mv, z_sd, z_rstd = (
            sem(n) for n in ("z_mm", "z_lo", "z_hi", "wa_mm", "r_lo", "r_hi", "wb_mm", "z_b",
                             "z_stats", "z_mv", "z_sd", "z_rstd"))
        z_norm, z_gain, z_bias = sem("z_norm"), sem("z_gain"), sem("z_bias")
        h3T_ps, h3T_done, d1_mm, d1_done, d2_mm, xb_done, o_sum, o_stats, o_mv, o_sd, o_rstd = (
            sem(n) for n in ("h3T_ps", "h3T_done", "d1_mm", "d1_done", "d2_mm", "xb_done", "o_sum",
                             "o_stats", "o_mv", "o_sd", "o_rstd"))
        o_norm, o_gain, o_bias, o_res, f_stats, f_mv, f_sd, f_rstd, f_done, out_done = (
            sem(n) for n in ("o_norm", "o_gain", "o_bias", "o_res", "f_stats", "f_mv", "f_sd",
                             "f_rstd", "f_done", "out_done"))

        def window(b):
            return pb[0:P, 2 * b:2 * b + 2, 0:C].rearrange("p r (b w) -> p r b w", w=W)

        def wait_apart(eng, s, value):
            eng.wait_ge(s, 1)
            eng.wait_ge(s, value)

        block = ctx.enter_context(nc.Block())

        @block.sync
        def _(sp):
            for s in (out_done,):
                sp.sem_inc(s, 16)
            for a, d in ((src_i, src), (dst_i, dst), (typ_i, typ)):
                sp.dma_start(a[:], d.rearrange("(g e) -> g e", g=G)).then_inc(edges_in, 16)
            sp.dma_start(xt[:], x_t[0]).then_inc(x_in, 16)
            with nc.allow_non_contiguous_dma(reason="vectors onto the partitions, 4 bytes each"):
                sp.dma_start(lnw[:], column(ln_w)).then_inc(consts_in, 16)
                sp.dma_start(g_c[:], column(g_in)).then_inc(consts_in, 16)
                sp.dma_start(b_c[:], column(b_in)).then_inc(consts_in, 16)
                sp.dma_start(b1_c[:], column(b1)).then_inc(consts_in, 16)
                sp.dma_start(bd1_c[:], column(bd1)).then_inc(consts_in, 16)
            sp.dma_start(b2_b[:], spread(b2)).then_inc(consts_in, 16)
            sp.dma_start(w_all[:, :, 0:F], w_root.rearrange("(k p) f -> p k f", p=128)).then_inc(w_in, 16)
            for r in range(R):
                sp.dma_start(w_all[:, :, (r + 1) * F:(r + 2) * F],
                             w_rel[r].rearrange("(k p) f -> p k f", p=128)).then_inc(w_in, 16)
            with sp.Fori(1, T) as t:
                sp.wait_ge(xn_ready, t)
                sp.dma_start(xt[:], x_t[bass.ds(t, 1)].rearrange("o p d -> (o p) d")).then_inc(x_in, 16)
            sp.wait_ge(xn_ready, T)
            sp.dma_start(xt[:], x_t[0]).then_inc(x_in, 16)
            sp.wait_ge(adj_done, 1)
            sp.wait_ge(proj_mm, 1 + T)
            sp.dma_start(wo_s[:, 0:2, :], wo[0:256].rearrange("(k p) d -> p k d", p=128)).then_inc(wo_in, 16)
            sp.dma_start(wo_s[0:FB[2], 2, :], wo[256:F]).then_inc(wo_in, 16)
            sp.dma_start(cb_b[:], spread(conv_b)).then_inc(wo_in, 16)
            with sp.Fori(1, T) as t:
                sp.wait_ge(res_done, t)
                sp.dma_start(xt[:], x_t[bass.ds(t, 1)].rearrange("o p d -> (o p) d")).then_inc(x_in, 16)
            sp.wait_ge(agg_mm, T)
            sp.wait_ge(adj_sum, T)
            sp.dma_start(w1_s[:], w1.rearrange("(k p) f -> p k f", p=128)).then_inc(w12_in, 16)
            sp.dma_start(w2_s[:], w2.rearrange("(k p) f -> p k f", p=128)).then_inc(w12_in, 16)
            sp.wait_ge(rel0_added, T)
            for a, d in ((bb_b, bb), (ng_b, ng), (nb_b, nb)):
                sp.dma_start(a[:], d.rearrange("l d -> (l d)").rearrange("(o d) -> o d", o=1)
                             .broadcast_to([P, L * HB]).rearrange("p (l d) -> p l d", l=L)).then_inc(rows_in, 16)
            for i in range(L):
                if i > 0:
                    sp.wait_ge(wb_mm, T * i)
                sp.dma_start(wa_s[:], wa[i].rearrange("(k p) f -> p k f", p=128)).then_inc(wab_in, 16)
                sp.dma_start(wb_s[:], wb[i].rearrange("(k p) f -> p k f", p=128)).then_inc(wab_in, 16)
                with nc.allow_non_contiguous_dma(reason="a vector onto the partitions, 4 bytes each"):
                    sp.dma_start(ba_c[:], column(ba[i])).then_inc(wab_in, 16)
                if i == 0:
                    sp.wait_ge(h_mm, 1 + T)
                    sp.dma_start(wd1_s[:], wd1.rearrange("(k p) f -> p k f", p=128)).then_inc(wd_in, 16)
                    sp.dma_start(wd2_s[:], wd2.rearrange("(k p) f -> p k f", p=128)).then_inc(wd_in, 16)
                    for a, d in ((bd2_b, bd2), (go_b, g_out), (bo_b, b_out)):
                        sp.dma_start(a[:], spread(d)).then_inc(wd_in, 16)
            with sp.Fori(0, T) as t:
                sp.wait_ge(f_done, 1 + t + 1)
                sp.dma_start(out_t[bass.ds(t, 1)].rearrange("o p d -> (o p) d"), ot[:]).then_inc(out_done, 16)
            sp.wait_ge(out_done, 16 + 16 * T)

        @block.gpsimd
        def _(pool):
            pool.iota(iota_r[:], [[1, 128]], base=0, channel_multiplier=0,
                      allow_small_or_imprecise_dtypes=True).then_inc(iotas, 1)
            pool.iota(iota_i[:], [[0, 1]], base=0, channel_multiplier=1,
                      allow_small_or_imprecise_dtypes=True).then_inc(iotas, 1)
            pool.iota(iota_l[:], [[1, P]], base=0, channel_multiplier=0,
                      allow_small_or_imprecise_dtypes=True).then_inc(iotas, 1)
            pool.iota(iota_c[:], [[1, R * C]], base=0, channel_multiplier=0,
                      allow_small_or_imprecise_dtypes=True).then_inc(iotas, 1)
            pool.memset(adj[:, 0], 0.0).then_inc(adj_zero, 1)
            pool.wait_ge(ln2_shift, 1)
            pool.wait_ge(adj_sum, T)
            for t in range(T):
                if t >= 2:
                    pool.wait_ge(xhT_ps, 2 * t - 2)
                pool.tensor_scalar(xh[:, t % 2], x1[:, t], small2[:, 0, t:t + 1], small2[:, 1, t:t + 1],
                                   ALU.mult, ALU.add).then_inc(xh_ready, 1)
            pool.wait_ge(wd_in, 80)
            with pool.Fori(0, T) as t:
                a = x1[:, bass.ds(t, 1)].rearrange("p o d -> p (o d)")
                pool.wait_ge(o_sum, 1 + t)
                pool.tensor_tensor(ot2[:], a, bd2_b[:], ALU.add).then_inc(xb_done, 1)

        @block.scalar
        def _(act):
            for s in (xnT_copied, y_copied, hT_lo, r1_done, d1_done,):
                act.sem_inc(s, 1)
            act.wait_ge(small_set, 4)
            act.activation(adj[:, 1].rearrange("p b d -> p (b d)"),
                           zero[:, 0:1].broadcast_to([P, T * ND]), ACT.Copy).then_inc(adj_zero, 1)

            def root_norm(t):
                act.wait_ge(x_in, (t + 1) * 16)
                act.activation(xn[:], xt[:], ACT.Square, accum_out=small1[:, 0:1]).then_inc(xn_sq, 1)
                act.wait_ge(xn_sq, t + 1)
                act.activation(small1[:, 1:2], small1[:, 0:1], ACT.Sqrt, bias=eps0[:, 0:1],
                               scale=1.0 / D).then_inc(xn_sd, 1)
                act.wait_ge(xn_rstd, t + 1)
                act.activation(xn[:], xt[:], ACT.Copy, scale=small1[:, 2:3]).then_inc(xn_ready, 1)

            def tile_of_1(t, last):
                for q in range(2):
                    act.wait_ge(xnT_ps, t * 2 + q + 1)
                    if q == 0:
                        act.wait_ge(proj_mm, 1 + t)
                    for i in range(4):
                        k = 4 * q + i
                        ins = act.activation(xnT[:, k], pb[:, 7, i * P:(i + 1) * P], ACT.Copy,
                                             scale=lnw[:, k:k + 1])
                    ins.then_inc(xnT_copied, 1)
                if not last:
                    root_norm(t + 1)
                wait_apart(act, proj_mm, 1 + t + 1)
                yt = y[:, bass.ds(t, 1)].rearrange("p o f -> p (o f)")
                act.copy(yt[:, 0:F], pb[0:P, 4, 0:F])
                act.copy(yt[:, F:2 * F], pb[0:P, 5, 0:F])
                act.copy(yt[:, 2 * F + 1:3 * F + 1], pb[0:P, 6, 0:F]).then_inc(y_copied, 1)

            act.wait_ge(consts_in, 16 * 6)
            root_norm(0)
            act.wait_ge(codes_ready, 1)
            with act.Fori(0, T - 1) as t:
                tile_of_1(t, False)
            tile_of_1(T - 1, True)

            def elu_parts_of(t):
                act.wait_ge(neg_part, t + 1)
                act.activation(ybuf[:, 2], ybuf[:, 1], ACT.Exp)
                act.activation(ybuf[:, 3], ybuf[:, 0], ACT.Relu).then_inc(elu_parts, 1)

            def turned(t):
                act.wait_ge(yT_ps, t + 1)
                act.wait_ge(wo_mm, 1 + t)
                act.copy(yT[:, 0:2].rearrange("p k n -> p (k n)"), pb[:, 4, 0:2 * P])
                act.copy(yT[0:FB[2], 2], pb[0:FB[2], 4, 2 * P:3 * P]).then_inc(yT_copied, 1)

            elu_parts_of(0)
            with act.Fori(0, T - 1) as t:
                turned(t)
                elu_parts_of(t + 1)
            turned(T - 1)

            act.wait_ge(res_mv, T)
            act.activation(small2[:, 0, 0:T], mv[:, :, 1], ACT.Sqrt, bias=epsc[:, 0:1]).then_inc(ln1_sd, 1)
            act.wait_ge(ln1_shift, 1)
            for t in range(T):
                act.activation(x1[:, t], x1[:, t], ACT.Identity, scale=small2[:, 0, t:t + 1],
                               bias=small2[:, 1, t:t + 1]).then_inc(x1_ready, 1)
            act.wait_ge(x1_mv, T)
            act.activation(small2[:, 0, 0:T], mv[:, :, 1], ACT.Sqrt, bias=epsc[:, 0:1]).then_inc(ln2_sd, 1)

            act.wait_ge(adj_sum, T)
            with act.Fori(0, T // 2) as c:
                act.wait_ge(r1_mm, 1 + c * K1)
                for u in range(2):
                    act.wait_ge(xhT_ps, c * 4 + 2 * u + 1)
                    for i in range(4):
                        ins = act.activation(hT[:, i, u * P:(u + 1) * P], pb[:, 2 * u, i * P:(i + 1) * P],
                                             ACT.Identity, scale=g_c[:, i:i + 1], bias=b_c[:, i:i + 1])
                    ins.then_inc(hT_lo, 1)
                act.wait_ge(h_mm, 1 + c * 2)
                for f in range(K1):
                    act.wait_ge(r1_mm, 1 + c * K1 + f + 1)
                    act.activation(r1T[:, f], pb[:, 4 + f % 2, 0:2 * P],
                                   ACT.Relu, bias=b1_c[:, f:f + 1]).then_inc(r1_done, 1)

            def layer(i):
                act.wait_ge(z_mm, i + 1)
                for c, (c0, n) in enumerate(CH):
                    act.copy(zT[:, 0, c0:c0 + n], pb[:, c, 0:n]).then_inc(z_lo, 1)
                for c, (c0, n) in enumerate(CH):
                    act.wait_ge(wa_mm, i * 6 + 2 * c + 1)
                    act.activation(rT[:, 0, c0:c0 + n], pb[:, c, 0:n], ACT.Relu,
                                   bias=ba_c[:, 0:1]).then_inc(r_lo, 1)
                for t in range(T):
                    act.wait_ge(z_mv, i * T + t + 1)
                    act.activation(small4[:, 2 + t % 2:3 + t % 2], mv4[:, t % 2, 1:2], ACT.Sqrt,
                                   bias=epsc[:, 0:1]).then_inc(z_sd, 1)

            with act.Fori(0, L) as i:
                layer(i)

            def out_norm(t):
                act.wait_ge(o_mv, t + 1)
                act.activation(small4[:, 4:5], mv4[:, 0, 1:2], ACT.Sqrt, bias=epsc[:, 0:1]).then_inc(o_sd, 1)
                act.wait_ge(f_mv, t + 1)
                act.activation(small4[:, 5:6], mv4[:, 1, 1:2], ACT.Sqrt, bias=epsc[:, 0:1]).then_inc(f_sd, 1)

            with act.Fori(0, T // 2) as c:
                act.wait_ge(d1_mm, 1 + c * K1)
                for u in range(2):
                    act.wait_ge(h3T_ps, c * 2 + u + 1)
                    act.copy(h3T[:, :, u * P:(u + 1) * P],
                             pb[:, 7 * u, 0:2 * P].rearrange("p (k n) -> p k n", k=K2)
                             ).then_inc(h3T_done, 1)
                act.wait_ge(d2_mm, 1 + c * 2)
                for f in range(K1):
                    act.wait_ge(d1_mm, 1 + c * K1 + f + 1)
                    act.activation(dT[:, f], pb[:, 1 + f % 2, 0:2 * P],
                                   ACT.Relu, bias=bd1_c[:, f:f + 1]).then_inc(d1_done, 1)
                for u in range(2):
                    out_norm(c * 2 + u)

        @block.tensor
        def _(pe):
            for s in (proj_mm, wo_mm, r1_mm, h_mm, d1_mm, d2_mm,):
                pe.sem_inc(s, 1)
            pe.wait_ge(small_set, 5)
            pe.wait_ge(edges_ready, 1)
            for f, a in enumerate((e_low, e_code, e_base, e_far)):
                for j in range(J):
                    pe.transpose(pb[0:P, f, j * G:(j + 1) * G], a[:, j * P:(j + 1) * P], ident[0:G, 0:G])
            for i in range(2):
                ins = pe.transpose(pb[0:1, 4, i * 128:i * 128 + G], gmin[:, i:i + 1], ident[0:G, 0:G])
            ins.then_inc(edges_ps, 1)

            def count(b):
                for j in range(J):
                    for r in range(R):
                        ins = pe.matmul(pb[0:P, 2 * b + r, 0:C], oh_low[:, b, j], oh_code[:, b, j, r * C:(r + 1) * C],
                                        start=(j == 0), stop=(j == J - 1))
                return ins

            pe.wait_ge(codes_ready, 1)
            pe.wait_ge(w_in, 48)
            share = {2: [0, 1], 3: [2], 4: [3, 4], 5: [5], 6: [6], 7: [7]}
            with pe.Fori(0, T) as t:
                for u in range(UG):
                    pe.wait_ge(onehots, t * UG + u + 1)
                    pe.wait_ge(counts_free, t * UG + u + 1)
                    count(u % 2).then_inc(counts_mm, 1)
                    if u < 2:
                        if u == 0:
                            pe.wait_ge(xn_ready, t + 1)
                        pe.wait_ge(xnT_copied, 1 + t * 2 + u)
                        for i in range(4):
                            k = 4 * u + i
                            ins = pe.transpose(pb[:, 7, i * P:(i + 1) * P], xn[:, k * 128:(k + 1) * 128],
                                               ident[0:P, 0:P])
                        ins.then_inc(xnT_ps, 1)
                    for k in share.get(u, ()):
                        if k == 0:
                            pe.wait_ge(y_copied, 1 + t)
                        if k % 4 == 0:
                            pe.wait_ge(xnT_copied, 1 + t * 2 + k // 4 + 1)
                        for n in range(3):
                            ins = pe.matmul(pb[0:P, 4 + n, 0:F], xnT[:, k], w_all[:, k, n * F:(n + 1) * F],
                                            start=(k == 0), stop=(k == KD - 1))
                        if k == KD - 1:
                            ins.then_inc(proj_mm, 1)

            far = pe.value_load(seln[0:1, 0:1], min_val=0, max_val=1)
            with pe.If(far > 0):
                with pe.Fori(0, NW * G) as i:
                    pe.wait_ge(s_onehots, i + 1)
                    count(0).then_inc(s_counts_mm, 1)

            def project(t):
                pe.wait_ge(elu_done, t + 1)
                f0 = 0
                for i, n in enumerate(FB):
                    ins = pe.transpose(pb[0:n, 4, i * P:(i + 1) * P], ybuf[:, 4, f0:f0 + n], ident[0:P, 0:P])
                    f0 += n
                ins.then_inc(yT_ps, 1)
                pe.wait_ge(yT_copied, t + 1)
                if t > 0:
                    pe.wait_ge(res_done, t)
                for q in range(2):
                    for i, n in enumerate(FB):
                        ins = pe.matmul(pb[0:P, 5 + q], yT[0:n, i], wo_s[0:n, i, q * 512:(q + 1) * 512],
                                        start=(i == 0), stop=(i == 2))
                ins.then_inc(wo_mm, 1)

            pe.wait_ge(adj_done, 1)
            pe.wait_ge(y_copied, 1 + T)
            for t in range(T):
                if t >= 2:
                    pe.wait_ge(pre_elu, t - 1)
                for s in range(T):
                    for r in range(R):
                        ins = pe.matmul(pb[0:P, 2 * (t % 2) + r, 0:F + 1], adj[:, r, s, t * P:(t + 1) * P],
                                        y[:, s, F + r * (F + 1):F + (r + 1) * (F + 1)],
                                        start=(s == 0), stop=(s == T - 1))
                ins.then_inc(agg_mm, 1)
                if t == 1:
                    pe.wait_ge(wo_in, 48)
                if t > 0:
                    project(t - 1)
            project(T - 1)

            pe.wait_ge(w12_in, 32)
            with pe.Fori(0, T // 2) as c:
                for u in range(2):
                    pe.wait_ge(xh_ready, c * 2 + u + 1)
                    pe.wait_ge(hT_lo, 1 + c * 2)
                    pe.wait_ge(hT_hi, 1 + c * 2)
                    for q in range(2):
                        for i in range(4):
                            k = 4 * q + i
                            ins = pe.transpose(pb[:, 2 * u + q, i * P:(i + 1) * P],
                                               xh[:, u, k * 128:(k + 1) * 128], ident[0:P, 0:P])
                        ins.then_inc(xhT_ps, 1)
                pe.wait_ge(hT_lo, 1 + c * 2 + 2)
                pe.wait_ge(hT_hi, 1 + c * 2 + 2)
                pe.wait_ge(r1_done, 1 + c * K1)
                for f in range(K1):
                    if f >= 2:
                        pe.wait_ge(r1_done, 1 + c * K1 + f - 1)
                    for k in range(KD):
                        ins = pe.matmul(pb[:, 4 + f % 2, 0:2 * P],
                                        w1_s[:, k, f * 128:(f + 1) * 128], hT[:, k],
                                        start=(k == 0), stop=(k == KD - 1))
                    ins.then_inc(r1_mm, 1)
                pe.wait_ge(r1_done, 1 + c * K1 + K1)
                pe.wait_ge(h_done, 1 + c * 2)
                for u in range(2):
                    for k in range(K1):
                        ins = pe.matmul(pb[0:P, 6 + u, 0:HB], r1T[:, k, u * P:(u + 1) * P], w2_s[:, k],
                                        start=(k == 0), stop=(k == K1 - 1))
                    ins.then_inc(h_mm, 1)

            def aggregate(s):
                for f in range(K2):
                    for c, (c0, n) in enumerate(CH):
                        ins = pe.matmul(pb[:, 3 * f + c, 0:n], h[:, s, f * 128:(f + 1) * 128],
                                        adj[:, 0, s, c0:c0 + n], start=(s == 0), stop=(s == T - 1))
                return ins

            def layer(i, last):
                pe.wait_ge(wab_in, i * 48 + 48)
                for c, (c0, n) in enumerate(CH):
                    pe.wait_ge(z_lo, i * 3 + c + 1)
                    pe.wait_ge(z_hi, i * 3 + c + 1)
                    for f in range(K2):
                        for k in range(K2):
                            ins = pe.matmul(pb[:, 3 * f + c, 0:n], wa_s[:, k, f * 128:(f + 1) * 128],
                                            zT[:, k, c0:c0 + n], start=(k == 0), stop=(k == K2 - 1))
                        ins.then_inc(wa_mm, 1)

                def second(t):
                    c = [c for c, (c0, n) in enumerate(CH) if c0 <= t * P < c0 + n][0]
                    pe.wait_ge(r_lo, i * 3 + c + 1)
                    pe.wait_ge(r_hi, i * 3 + c + 1)
                    pe.wait_ge(z_b, 1 + i * T + max(t - 1, 0))
                    for k in range(K2):
                        ins = pe.matmul(pb[0:P, 6 + t % 2, 0:HB], rT[:, k, t * P:(t + 1) * P], wb_s[:, k],
                                        start=(k == 0), stop=(k == K2 - 1))
                    ins.then_inc(wb_mm, 1)

                for t in range(T + 2):
                    if t < T:
                        second(t)
                    if t >= 2 and not last:
                        if t == 2:
                            pe.wait_ge(r_lo, i * 3 + 3)
                            pe.wait_ge(r_hi, i * 3 + 3)
                        pe.wait_ge(h_done, 1 + (i + 1) * T + t - 1)
                        ins = aggregate(t - 2)
                if not last:
                    ins.then_inc(z_mm, 1)

            for s in range(T):
                pe.wait_ge(h_done, 1 + s + 1)
                ins = aggregate(s)
            ins.then_inc(z_mm, 1)
            with pe.Fori(0, L - 1) as i:
                layer(i, False)
            layer(L - 1, True)

            pe.wait_ge(h_done, 1 + (L + 1) * T)
            pe.wait_ge(wd_in, 80)
            for c in range(T // 2):
                pe.wait_ge(h3T_done, c * 2)
                for u in range(2):
                    for k in range(K2):
                        ins = pe.transpose(pb[:, 7 * u, k * P:(k + 1) * P],
                                           h[:, 2 * c + u, k * 128:(k + 1) * 128], ident[0:P, 0:P])
                    ins.then_inc(h3T_ps, 1)
                pe.wait_ge(h3T_done, c * 2 + 2)
                pe.wait_ge(d1_done, 1 + c * K1)
                for f in range(K1):
                    if f >= 2:
                        pe.wait_ge(d1_done, 1 + c * K1 + f - 1)
                    for k in range(K2):
                        ins = pe.matmul(pb[:, 1 + f % 2, 0:2 * P],
                                        wd1_s[:, k, f * 128:(f + 1) * 128], h3T[:, k],
                                        start=(k == 0), stop=(k == K2 - 1))
                    ins.then_inc(d1_mm, 1)
                pe.wait_ge(d1_done, 1 + c * K1 + K1)
                pe.wait_ge(o_sum, 1 + c * 2)
                for u in range(2):
                    for q in range(2):
                        for k in range(K1):
                            ins = pe.matmul(pb[0:P, 3 + 2 * u + q], dT[:, k, u * P:(u + 1) * P],
                                            wd2_s[:, k, q * 512:(q + 1) * 512],
                                            start=(k == 0), stop=(k == K1 - 1))
                    ins.then_inc(d2_mm, 1)

        @block.vector
        def _(dve):
            for s in (hT_hi, h_done, z_b, o_sum, f_done,):
                dve.sem_inc(s, 1)
            dve.memset(eps0[:], EPS0).then_inc(small_set, 1)
            dve.memset(epsc[:], EPS).then_inc(small_set, 1)
            dve.memset(zero[:], 0.0).then_inc(small_set, 1)
            dve.memset(mini[:], 0).then_inc(small_set, 1)
            dve.wait_ge(iotas, 4)
            dve.tensor_scalar(ident[:], iota_r[:], iota_i[:, 0:1], None, ALU.is_equal).then_inc(small_set, 1)

            steps = [0]

            def step(ins):
                ins.then_inc(prep, 1)
                steps[0] += 1
                dve.wait_ge(prep, steps[0])

            dve.wait_ge(edges_in, 48)
            dve.tensor_copy(e_low[:], src_i[:])
            dve.tensor_copy(e_base[:], typ_i[:])
            step(dve.tensor_copy(e_far[:], dst_i[:]))
            step(dve.tensor_reduce(gmin[:, 0:1], e_far[:], AX.X, ALU.min))
            dve.tensor_scalar(e_rel[:], e_far[:], gmin[:, 0:1], None, ALU.subtract)
            step(dve.tensor_scalar(e_blk[:], e_low[:], float(P), None, ALU.is_ge))
            for k in range(2, T):
                step(dve.scalar_tensor_tensor(e_blk[:], e_low[:], float(P * k), e_blk[:], ALU.is_ge, ALU.add))
            dve.scalar_tensor_tensor(e_low[:], e_blk[:], -float(P), e_low[:], ALU.mult, ALU.add)
            step(dve.tensor_scalar(e_base[:], e_base[:], float(C), None, ALU.mult))
            step(dve.scalar_tensor_tensor(e_base[:], e_blk[:], float(W), e_base[:], ALU.mult, ALU.add))
            step(dve.tensor_scalar(e_blk[:], e_rel[:], float(W), None, ALU.is_ge))
            dve.tensor_reduce(gmin[:, 1:2], e_blk[:], AX.X, ALU.max)
            dve.scalar_tensor_tensor(e_far[:], e_blk[:], -float(FAR), e_far[:], ALU.mult, ALU.add)
            step(dve.scalar_tensor_tensor(e_rel[:], e_blk[:], float(FAR), e_rel[:], ALU.mult, ALU.add))
            dve.tensor_scalar(e_far[:], e_far[:], float(FAR), None, ALU.add)
            dve.tensor_tensor(e_code[:], e_rel[:], e_base[:], ALU.add).then_inc(edges_ready, 1)
            dve.memset(edgeT[:], 0.0).then_inc(prep, 1)
            steps[0] += 1
            dve.wait_ge(prep, steps[0])
            dve.wait_ge(edges_ps, 1)
            for f in range(4):
                dve.tensor_copy(edgeT[:, f, :, 0:G], pb[0:P, f, 0:J * G].rearrange("p (j g) -> p j g", j=J))
            dve.tensor_copy(mini[0:1, 0:G], pb[0:1, 4, 0:G])
            dve.memset(y[:, :, 2 * F:2 * F + 1], 1.0)
            dve.memset(y[:, :, 3 * F + 1:3 * F + 2], 1.0)
            step(dve.tensor_reduce(small1[0:1, 4:5], pb[0:1, 4, 128:128 + G], AX.X, ALU.max))
            dve.tensor_copy(seln[0:1, 0:1], small1[0:1, 4:5]).then_inc(codes_ready, 1)
            for _i in range(2):
                dve.memset(small1[:, 5 + _i:6 + _i], 0.0).then_inc(counts_free, 1)
            dve.wait_ge(codes_ready, 1)

            def build(g, b, low, code):
                for j in range(J):
                    dve.tensor_scalar(oh_low[:, b, j], iota_l[:], low(j, g), None, ALU.is_equal)
                for j in range(J):
                    ins = dve.tensor_scalar(oh_code[:, b, j], iota_c[:], code(j, g), None, ALU.is_equal)
                return ins

            def low_of(j, g):
                return edgeT[:, 0, j, bass.ds(g, 1)]

            def code_of(j, g):
                return edgeT[:, 1, j, bass.ds(g, 1)]

            for g in range(2):
                build(g, g, low_of, code_of).then_inc(onehots, 1)
            dve.wait_ge(adj_zero, 2)
            dve.wait_ge(xn_sd, 1)
            dve.reciprocal(small1[:, 2:3], small1[:, 1:2]).then_inc(xn_rstd, 1)

            def tile_of_1(t, last):
                base = nc.values_load_multi_w_load_instructions(
                    mini[0:1, bass.ds(t * UG, UG)], engines=[mybir.EngineType.DVE], min_val=0, max_val=N - 1)[1]
                for u in range(UG):
                    if u == 4 and not last:
                        dve.wait_ge(xn_sd, t + 2)
                        dve.reciprocal(small1[:, 2:3], small1[:, 1:2]).then_inc(xn_rstd, 1)
                    g = t * UG + u
                    dve.wait_ge(counts_mm, g + 1)
                    dve.wait_ge(counts_free, g + 2)
                    place = adj[:, :, :, bass.ds(base[u], W)]
                    dve.tensor_tensor(place, place, window(u % 2), ALU.add).then_inc(counts_free, 1)
                    build(g + 2, u % 2, low_of, code_of).then_inc(onehots, 1)

            with dve.Fori(0, T - 1) as t:
                tile_of_1(t, False)
            tile_of_1(T - 1, True)

            dve.wait_ge(counts_free, G + 2)
            dve.wait_ge(onehots, G + 2)
            far = dve.value_load(seln[0:1, 0:1], min_val=0, max_val=1)
            with dve.If(far > 0):
                dist = edgeT[:, 3]
                with dve.Fori(0, NW) as w:
                    dve.tensor_scalar(maskS[:, 0], dist, 0.0, float(FAR), ALU.is_lt, ALU.mult)
                    dve.tensor_scalar(maskS[:, 1], dist, float(W), float(FAR), ALU.is_ge, ALU.mult)
                    dve.tensor_tensor(codeS[:], dist, edgeT[:, 2], ALU.add).then_inc(s_codes, 1)
                    dve.wait_ge(s_codes, w * 4 + 1)
                    dve.tensor_tensor(codeS[:], codeS[:], maskS[:, 0], ALU.add).then_inc(s_codes, 1)
                    dve.wait_ge(s_codes, w * 4 + 2)
                    dve.tensor_tensor(codeS[:], codeS[:], maskS[:, 1], ALU.add).then_inc(s_codes, 1)
                    dve.tensor_scalar(dist, dist, -float(W), None, ALU.add).then_inc(s_codes, 1)
                    with dve.Fori(0, G) as g:
                        dve.wait_ge(s_codes, w * 4 + 4)
                        build(g, 0, low_of, lambda j, g: codeS[:, j, bass.ds(g, 1)]).then_inc(s_onehots, 1)
                        dve.wait_ge(s_counts_mm, w * G + g + 1)
                        place = adj[:, :, :, bass.ds(w * W, W)]
                        dve.tensor_tensor(place, place, window(0), ALU.add).then_inc(s_added, 1)
                        dve.wait_ge(s_added, w * G + g + 1)
            dve.memset(small1[:, 7:8], 0.0).then_inc(adj_done, 1)

            dve.wait_ge(wo_in, 48)
            dve.wait_ge(y_copied, 1 + T)
            b0, b1_, b2_, b3_, b4_ = (ybuf[:, i] for i in range(5))

            def relations(t, b, first):
                dve.tensor_tensor(b0, y[:, t, 0:F], cb_b[:], ALU.add).then_inc(root_b, 1)
                dve.wait_ge(agg_mm, t + 1)
                dve.tensor_scalar(rc[:, :, 0:1], pb[0:P, 2 * b:2 * b + 2, F:F + 1], 1.0, None, ALU.max).then_inc(cnt_max, 1)
                dve.wait_ge(cnt_max, t + 1)
                dve.reciprocal(rc[:, :, 1:2], rc[:, :, 0:1]).then_inc(cnt_rcp, 1)
                dve.wait_ge(cnt_rcp, t + 1)
                dve.wait_ge(root_b, t + 1)
                dve.scalar_tensor_tensor(b0, pb[0:P, 2 * b, 0:F], rc[:, 0, 1:2], b0, ALU.mult, ALU.add).then_inc(rel0_added, 1)
                dve.wait_ge(rel0_added, t + 1)
                dve.scalar_tensor_tensor(b0, pb[0:P, 2 * b + 1, 0:F], rc[:, 1, 1:2], b0, ALU.mult, ALU.add).then_inc(pre_elu, 1)
                dve.wait_ge(pre_elu, t + 1)
                dve.tensor_scalar(b1_, b0, 0.0, None, ALU.min).then_inc(neg_part, 1)
                cols = slice(t * P, (t + 1) * P)
                dve.tensor_tensor(adj[:, 0, :, cols], adj[:, 0, :, cols], adj[:, 1, :, cols], ALU.add).then_inc(adj_sum, 1)
                dve.wait_ge(elu_parts, t + 1)
                if t > 0:
                    dve.wait_ge(yT_ps, t)
                dve.scalar_tensor_tensor(b4_, b2_, -1.0, b3_, ALU.add, ALU.add).then_inc(elu_done, 1)
                dve.wait_ge(adj_sum, t + 1)
                dve.tensor_tensor(adj[:, 0, t, cols], adj[:, 0, t, cols], ident[0:P, 0:P], ALU.add).then_inc(adj_self, 1)

            def residual(t):
                dve.wait_ge(wo_mm, 1 + t + 1)
                dve.wait_ge(x_in, 16 * (T + t + 1))
                dve.scalar_tensor_tensor(x1[:, t], xt[:], 2.0, pb[0:P, 5:7].rearrange("p a b -> p (a b)"),
                                         ALU.mult, ALU.add).then_inc(res_done, 1)
                dve.wait_ge(res_done, t + 1)
                dve.bn_stats(st2[:, 0], x1[:, t, 0:512])
                dve.bn_stats(st2[:, 1], x1[:, t, 512:D]).then_inc(res_stats, 1)
                dve.wait_ge(res_stats, t + 1)
                dve.bn_aggr(mv[:, t], st2[:].rearrange("p a b -> p (a b)")).then_inc(res_mv, 1)
                dve.wait_ge(res_mv, t + 1)

            for t in range(T):
                relations(t, t % 2, t == 0)
                if t > 0:
                    residual(t - 1)
            residual(T - 1)

            def shift(sd, rstd, done):
                dve.wait_ge(sd, 1)
                dve.reciprocal(small2[:, 0, 0:T], small2[:, 0, 0:T]).then_inc(rstd, 1)
                dve.wait_ge(rstd, 1)
                dve.scalar_tensor_tensor(small2[:, 1, 0:T], mv[:, :, 0], -1.0, small2[:, 0, 0:T],
                                         ALU.mult, ALU.mult).then_inc(done, 1)

            shift(ln1_sd, ln1_rstd, ln1_shift)
            dve.wait_ge(ln1_shift, 1)
            for t in range(T):
                dve.wait_ge(x1_ready, t + 1)
                dve.bn_stats(st2[:, 0], x1[:, t, 0:512])
                dve.bn_stats(st2[:, 1], x1[:, t, 512:D]).then_inc(x1_stats, 1)
                dve.wait_ge(x1_stats, t + 1)
                dve.bn_aggr(mv[:, t], st2[:].rearrange("p a b -> p (a b)")).then_inc(x1_mv, 1)
                dve.wait_ge(x1_mv, t + 1)
            shift(ln2_sd, ln2_rstd, ln2_shift)

            with dve.Fori(0, T // 2) as c:
                dve.wait_ge(r1_mm, 1 + c * K1)
                for u in range(2):
                    dve.wait_ge(xhT_ps, c * 4 + 2 * u + 2)
                    for i in range(4):
                        ins = dve.tensor_scalar(hT[:, 4 + i, u * P:(u + 1) * P], pb[:, 2 * u + 1, i * P:(i + 1) * P],
                                                g_c[:, 4 + i:5 + i], b_c[:, 4 + i:5 + i], ALU.mult, ALU.add)
                    ins.then_inc(hT_hi, 1)
                for u in range(2):
                    dve.wait_ge(h_mm, 1 + c * 2 + u + 1)
                    dve.tensor_tensor(h[:, bass.ds(c * 2 + u, 1)].rearrange("p o d -> p (o d)"),
                                      pb[0:P, 6 + u, 0:HB], b2_b[:], ALU.add).then_inc(h_done, 1)

            dve.wait_ge(rows_in, 48)

            def row(a, i):
                return a[:, bass.ds(i, 1)].rearrange("p o d -> p (o d)")

            def layer(i):
                dve.wait_ge(z_mm, i + 1)
                for c, (c0, n) in enumerate(CH):
                    dve.tensor_copy(zT[:, 1, c0:c0 + n], pb[:, 3 + c, 0:n]).then_inc(z_hi, 1)
                for c, (c0, n) in enumerate(CH):
                    dve.wait_ge(wa_mm, i * 6 + 2 * c + 2)
                    dve.tensor_scalar(rT[:, 1, c0:c0 + n], pb[:, 3 + c, 0:n],
                                      ba_c[:, 1:2], 0.0,
                                      ALU.add, ALU.max).then_inc(r_hi, 1)

                def stats(t):
                    v = i * T + t + 1
                    dve.wait_ge(wb_mm, v)
                    dve.tensor_tensor(zt[:, t % 2], pb[0:P, 6 + t % 2, 0:HB], row(bb_b, i), ALU.add).then_inc(z_b, 1)
                    dve.wait_ge(z_b, 1 + v)
                    dve.bn_stats(st4[:, t % 2], zt[:, t % 2]).then_inc(z_stats, 1)
                    wait_apart(dve, z_stats, v)
                    dve.bn_aggr(mv4[:, t % 2], st4[:, t % 2]).then_inc(z_mv, 1)

                def update(t):
                    v = i * T + t + 1
                    dve.wait_ge(z_sd, v)
                    dve.reciprocal(small4[:, t % 2:t % 2 + 1], small4[:, 2 + t % 2:3 + t % 2]).then_inc(z_rstd, 1)
                    dve.wait_ge(z_rstd, v)
                    dve.tensor_scalar(zt[:, 2], zt[:, t % 2], mv4[:, t % 2, 0:1], small4[:, t % 2:t % 2 + 1],
                                      ALU.subtract, ALU.mult).then_inc(z_norm, 1)
                    dve.wait_ge(z_norm, v)
                    dve.tensor_tensor(zt[:, 3], zt[:, 2], row(ng_b, i), ALU.mult).then_inc(z_gain, 1)
                    dve.wait_ge(z_gain, v)
                    dve.tensor_tensor(zt[:, 3], zt[:, 3], row(nb_b, i), ALU.add).then_inc(z_bias, 1)
                    dve.wait_ge(z_bias, v)
                    dve.scalar_tensor_tensor(h[:, t], zt[:, 3], 0.0, h[:, t], ALU.max, ALU.add).then_inc(h_done, 1)

                stats(0)
                for t in range(T):
                    if t + 1 < T:
                        stats(t + 1)
                    update(t)

            with dve.Fori(0, L) as i:
                layer(i)

            def chain(ins, s, t):
                ins.then_inc(s, 1)
                wait_apart(dve, s, t + 1)

            def stats_of(a, m, s_stats, s_mv, t):
                dve.bn_stats(st2[:, 0], a[:, 0:512])
                chain(dve.bn_stats(st2[:, 1], a[:, 512:D]), s_stats, t)
                dve.bn_aggr(mv4[:, m], st2[:].rearrange("p a b -> p (a b)")).then_inc(s_mv, 1)

            with dve.Fori(0, T // 2) as c:
                for u in range(2):
                    t = c * 2 + u
                    dve.wait_ge(d2_mm, 1 + t + 1)
                    dve.wait_ge(xb_done, t + 1)
                    dve.wait_ge(f_done, 1 + t)
                    chain(dve.tensor_tensor(ot3[:], pb[0:P, 3 + 2 * u:5 + 2 * u].rearrange("p a b -> p (a b)"), ot2[:],
                                            ALU.add), o_sum, t + 1)
                    stats_of(ot3, 0, o_stats, o_mv, t)
                    dve.wait_ge(o_sd, t + 1)
                    chain(dve.reciprocal(small4[:, 6:7], small4[:, 4:5]), o_rstd, t)
                    chain(dve.tensor_scalar(ot3[:], ot3[:], mv4[:, 0, 0:1], small4[:, 6:7], ALU.subtract, ALU.mult), o_norm, t)
                    chain(dve.tensor_tensor(ot3[:], ot3[:], go_b[:], ALU.mult), o_gain, t)
                    chain(dve.tensor_tensor(ot3[:], ot3[:], bo_b[:], ALU.add), o_bias, t)
                    chain(dve.tensor_tensor(ot3[:], ot3[:], x1[:, bass.ds(t, 1)].rearrange("p o d -> p (o d)"), ALU.add), o_res, t)
                    stats_of(ot3, 1, f_stats, f_mv, t)
                    dve.wait_ge(f_sd, t + 1)
                    chain(dve.reciprocal(small4[:, 7:8], small4[:, 5:6]), f_rstd, t)
                    dve.wait_ge(out_done, 16 + t * 16)
                    dve.tensor_scalar(ot[:], ot3[:], mv4[:, 1, 0:1], small4[:, 7:8], ALU.subtract,
                                      ALU.mult).then_inc(f_done, 1)


_INS = ['x', 'src', 'dst', 'edge_type_2', 'L0_gnn_ln_weight', 'L0_gnn_W_rel', 'L0_gnn_W_root',
        'L0_gnn_conv_bias', 'L0_gnn_wo_weight', 'L1_gnn_ln_in_g', 'L1_gnn_ln_in_b', 'L1_gnn_W1',
        'L1_gnn_b1', 'L1_gnn_W2', 'L1_gnn_b2', 'L1_gnn_layer_Wa', 'L1_gnn_layer_ba',
        'L1_gnn_layer_Wb', 'L1_gnn_layer_bb', 'L1_gnn_layer_ng', 'L1_gnn_layer_nb', 'L1_gnn_Wd1',
        'L1_gnn_bd1', 'L1_gnn_Wd2', 'L1_gnn_bd2', 'L1_gnn_out_g', 'L1_gnn_out_b']


def kernel(**inputs):
    import numpy as _np
    import concourse.bacc as _bacc
    from concourse import mybir as _mybir
    from concourse.bass_utils import run_bass_kernel_spmd as _run

    nc = _bacc.Bacc("TRN2", target_bir_lowering=False, num_devices=1)
    arrays, args = {}, []
    for name in _INS:
        a = _np.ascontiguousarray(inputs[name])
        arrays[f"in_{name}"] = a
        args.append(nc.dram_tensor(f"in_{name}", a.shape, _mybir.dt.from_np(a.dtype), kind="ExternalInput").ap())
    out = nc.dram_tensor("out_x", (N, D), F32, kind="ExternalOutput").ap()
    graph_kernel(nc, *args, out)
    r = _run(nc, [arrays], core_ids=[0])
    return r.results[0]["out_x"]
```

```python
from contextlib import ExitStack

import concourse.bass as bass
from concourse import mybir

ALU = mybir.AluOpType
ACT = mybir.ActivationFunctionType
AX = mybir.AxisListType
F32 = mybir.dt.float32
F32R = mybir.dt.float32r
F16 = mybir.dt.float16
BF16 = mybir.dt.bfloat16
I32 = mybir.dt.int32

N, D, E = 1250, 1024, 40000
P = 125
T = N // P
KD = D // 128
R, F = 2, 286
FW = 3 * F
FB = [128, 128, F - 256]
J = 4
G = E // (P * J)
GP = G + 4
W = 24
NW = -(-N // W)
C = T * W
ND = N + 32
H1, HB, L = 512, 256, 3
K1, K2 = H1 // 128, HB // 128
EXACT = 4096
FAR = 4096
ROUND = 1.5 * 2 ** 23
UG = G // T
CH = [(0, 500), (500, 500), (1000, 250)]
LAG = 3
EPS0, EPS = 1e-6, 1e-5


def graph_kernel(nc, x, src, dst, typ, ln_w, w_rel, w_root, conv_b, wo, g_in, b_in, w1, b1, w2, b2,
                 wa, ba, wb, bb, ng, nb, wd1, bd1, wd2, bd2, g_out, b_out, out):
    with ExitStack() as ctx:
        top = [16512]

        def at(off, name, shape, dt):
            return nc.alloc_sbuf_tensor_at(name, shape, dt, offset=off)

        def size(shape, dt):
            n = 2 if dt in (F16, BF16) else 4
            for k in shape[1:]:
                n *= k
            return -(-n // 32) * 32

        def stack(base, items):
            got = []
            for name, shape, dt in items:
                got.append(at(base, name, shape, dt))
                base += size(shape, dt)
            return got, base

        (adj, ident, eps0, epsc, ones, xt, seln, bign, deg, degmax, rs0, zero, rc), base = stack(top[0], [
            ("adj", [P, R, T, ND], F32), ("ident", [128, 128], F32), ("eps0", [P, 1], F32),
            ("epsc", [P, 1], F32), ("ones", [P, 1], F32), ("xt", [P, D], F32), ("seln", [1, 2], I32), ("bign", [1, 2], I32), ("deg", [P, T], F32), ("degmax", [P, 2], F32), ("rs0", [P, 1], F32), ("zero", [P, 1], F32), ("rc", [P, 2, 2], F32)])
        y_base = base
        (y,), base = stack(base, [("y", [P, T, FW + 2], F32)])
        rows = [(n, [G, J * P], d) for n, d in (
            ("src_i", I32), ("dst_i", I32), ("typ_i", I32), ("e_low", F32), ("e_code", F32),
            ("e_base", F32), ("e_far", F32), ("e_rel", F32))]
        (src_i, dst_i, typ_i, e_low, e_code, e_base, e_far, e_rel, e_blk, gmin), end = stack(
            y_base, rows + [("e_blk", [G, J * P], F32), ("gmin", [G, 2], F32)])
        assert end <= base
        p1 = base
        (w_all, xn, xnT, oh_low, oh_code, iota_c, iota_l, iota_r, iota_i, edgeT, codeS, maskS, lnw,
         mini, small1), end1 = stack(p1, [
             ("w_all", [128, KD, FW], F32), ("xn", [P, D], F32), ("xnT", [128, KD, P], F32),
             ("oh_low", [P, 2, J, P], BF16), ("oh_code", [P, 2, J, R * C], BF16),
             ("iota_c", [P, R * C], F16), ("iota_l", [P, P], F16), ("iota_r", [128, 128], F32),
             ("iota_i", [128, 1], F32), ("edgeT", [P, 4, J, GP], F32), ("codeS", [P, J, GP], F32),
             ("maskS", [P, 2, J, GP], F32), ("lnw", [128, KD], F32), ("mini", [1, GP], I32),
             ("small1", [P, 8], F32)])
        (x1, wo_s, cb_b, ybuf, yT, mv, small2, st2), end2 = stack(p1, [
            ("x1", [P, T, D], F32), ("wo_s", [128, 3, D], F32), ("cb_b", [P, F], F32),
            ("ybuf", [P, 5, F], F32), ("yT", [128, 3, P], F32), ("mv", [P, T, 4], F32),
            ("small2", [P, 4, T + 2], F32), ("st2", [P, 2, 6], F32)])
        adj1 = top[0] + size([P, T, ND], F32)
        adj1_end = top[0] + size([P, R, T, ND], F32)
        (w1_s, w2_s, xh, hT, r1T), end3 = stack(adj1, [
            ("w1_s", [128, KD, H1], F32), ("w2_s", [128, K1, HB], F32), ("xh", [P, 2, D], F32),
            ("hT", [128, KD, 2 * P], F32), ("r1T", [128, K1, 2 * P], F32)])
        (h_hi, h_lo), end = stack(adj1, [("h_hi", [P, T, HB], F32R), ("h_lo", [P, T, HB], F32R)])
        wd_base = end
        (wd1_s, wd2_s), end = stack(wd_base, [("wd1_s", [128, K2, H1], F32), ("wd2_s", [128, K1, D], F32)])
        z_base = max(end, end3)
        (zT,), end = stack(z_base, [("zT", [128, K2, N], F32)])
        assert end <= adj1_end, (end, adj1_end)
        adj_r = at(top[0], "adj_r", [P, T, ND], F32R)
        (dT, h3T, x_bd), end5 = stack(adj1, [("dT", [128, K1, 2 * P], F32), ("h3T", [128, K2, 2 * P], F32),
                                             ("x_bd", [P, 2, D], F32)])
        assert end5 <= wd_base
        (h, wa_s, wb_s, rT, bb_b, ng_b, nb_b), end4 = stack(y_base, [
            ("h", [P, T, HB], F32), ("wa_s", [128, K2, HB], F32), ("wb_s", [128, K2, HB], F32),
            ("rT", [128, K2, N], F32), ("bb_b", [P, L, HB], F32), ("ng_b", [P, L, HB], F32),
            ("nb_b", [P, L, HB], F32)])
        (zt, b2_b, g_c, b_c, b1_c, ba_c, bd1_c, st4, small4, mv4, mv5), end4b = stack(max(end1, end2), [
            ("zt", [P, 5, HB], F32), ("b2_b", [P, HB], F32), ("g_c", [128, KD], F32), ("b_c", [128, KD], F32),
            ("b1_c", [128, K1], F32), ("ba_c", [128, K2], F32), ("bd1_c", [128, K1], F32),
            ("st4", [P, 2, 6], F32), ("small4", [P, 8], F32), ("mv4", [P, 2, 2], F32),
            ("mv5", [P, 2, 2], F32)])
        rT_base = y_base + size([P, T, HB], F32) + 2 * size([P, K2, HB], F32)
        x_last = at(max(end1, end2), "x_last", [P, D], F32)
        assert end4 <= p1, (end4, p1)
        assert end4b <= nc.sbuf_usable_end, (end1, end2, end4b)
        (bd2_b, go_b, bo_b, ot, sd5, rs5, st5), end5b = stack(p1 + size([P, T, D], F32), [
            ("bd2_b", [P, D], F32), ("go_b", [P, D], F32), ("bo_b", [P, D], F32), ("ot", [P, 2, D], F32),
            ("sd5", [P, 2, 2], F32), ("rs5", [P, 2, 2], F32), ("st5", [P, 2, 2, 6], F32)])
        x_bo = at(z_base, "x_bo", [P, 2, D], F32)
        s5 = at(rT_base, "s5", [P, 2, D], F32)
        assert end5b <= max(end1, end2)

        pb = ctx.enter_context(nc.psum_tensor("banks", [128, 8, 512], F32))

        def sem(name):
            return ctx.enter_context(nc.semaphore(name))

        def tiled(a):
            return a.rearrange("(t p) d -> t p d", p=P)

        def column(a):
            return a.rearrange("(k p) -> p k", p=128)

        def spread(a):
            return a.rearrange("(o d) -> o d", o=1).broadcast_to([P, a.shape[0]])

        x_t, out_t = tiled(x), tiled(out)

        consts_in, edges_in, x_in, w_in = sem("consts_in"), sem("edges_in"), sem("x_in"), sem("w_in")
        wo_in, w2_in, wab_in, wd_in, rows_in = (sem("wo_in"), sem("w2_in"), sem("wab_in"),
                                                sem("wd_in"), sem("rows_in"))
        w1_in = [sem(f"w1_in{f}") for f in range(K1)]
        iotas, adj_zero, small_set = sem("iotas"), sem("adj_zero"), sem("small_set")
        prep, edges_ready, edges_ps, codes_ready = (sem("prep"), sem("edges_ready"), sem("edges_ps"),
                                                    sem("codes_ready"))
        onehots, counts_mm, counts_free = sem("onehots"), sem("counts_mm"), sem("counts_free")
        xn_sq, xn_sd, xn_rstd, xn_ready = sem("xn_sq"), sem("xn_sd"), sem("xn_rstd"), sem("xn_ready")
        xnT_ps, xnT_copied, proj_mm, y_copied = (sem("xnT_ps"), sem("xnT_copied"), sem("proj_mm"),
                                                 sem("y_copied"))
        s_codes, s_onehots, s_counts_mm, s_added = (sem("s_codes"), sem("s_onehots"),
                                                    sem("s_counts_mm"), sem("s_added"))
        adj_done = sem("adj_done")
        agg_mm, root_b, cnt_max, cnt_rcp, rel0_added, pre_elu, neg_part, elu_parts, elu_done = (
            sem(n) for n in ("agg_mm", "root_b", "cnt_max", "cnt_rcp", "rel0_added", "pre_elu",
                             "neg_part", "elu_parts", "elu_done"))
        adj_sum, adj_self, yT_ps, yT_copied, wo_mm, res_done, res_stats, res_mv = (
            sem(n) for n in ("adj_sum", "adj_self", "yT_ps", "yT_copied", "wo_mm", "res_done",
                             "res_stats", "res_mv"))
        ln1_sd, ln1_rstd, ln1_shift, x1_ready, x1_stats, x1_mv, ln2_sd, ln2_rstd, ln2_shift = (
            sem(n) for n in ("ln1_sd", "ln1_rstd", "ln1_shift", "x1_ready", "x1_stats", "x1_mv",
                             "ln2_sd", "ln2_rstd", "ln2_shift"))
        xh_ready, xhT_ps, hT_lo, hT_hi, r1_mm, r1_done, h_mm, h_done = (
            sem(n) for n in ("xh_ready", "xhT_ps", "hT_lo", "hT_hi", "r1_mm", "r1_done", "h_mm",
                             "h_done"))
        z_mm, z_lo, z_hi, wa_mm, r_lo, r_hi, wb_mm, z_b, z_stats, z_mv, z_sd, z_rstd = (
            sem(n) for n in ("z_mm", "z_lo", "z_hi", "wa_mm", "r_lo", "r_hi", "wb_mm", "z_b",
                             "z_stats", "z_mv", "z_sd", "z_rstd"))
        z_gain, z_bias = sem("z_gain"), sem("z_bias")
        hi_done, lo_done, adj_exact = sem("hi_done"), sem("lo_done"), sem("adj_exact")
        deg_sum, deg_ps, deg_set, big_ready = sem("deg_sum"), sem("deg_ps"), sem("deg_set"), sem("big_ready")
        h3T_ps, h3T_done, d1_mm, d1_done, d2_mm, xb_done, o_sum, o_stats, o_mv, o_sd, o_rstd = (
            sem(n) for n in ("h3T_ps", "h3T_done", "d1_mm", "d1_done", "d2_mm", "xb_done", "o_sum",
                             "o_stats", "o_mv", "o_sd", "o_rstd"))
        o_norm, o_gain, o_bias, o_res, f_stats, f_mv, f_sd, f_rstd, f_done, out_done, xo_done = (
            sem(n) for n in ("o_norm", "o_gain", "o_bias", "o_res", "f_stats", "f_mv", "f_sd",
                             "f_rstd", "f_done", "out_done", "xo_done"))

        def window(b):
            return pb[0:P, b, 0:R * C].rearrange("p (r b w) -> p r b w", r=R, w=W)

        def wait_apart(eng, s, value):
            eng.wait_ge(s, 1)
            eng.wait_ge(s, value)

        block = ctx.enter_context(nc.Block())

        @block.sync
        def _(sp):
            for s in (out_done,):
                sp.sem_inc(s, 16)
            for a, d in ((src_i, src), (dst_i, dst), (typ_i, typ)):
                sp.dma_start(a[:], d.rearrange("(g e) -> g e", g=G)).then_inc(edges_in, 16)
            sp.dma_start(xt[:], x_t[0]).then_inc(x_in, 16)
            with nc.allow_non_contiguous_dma(reason="vectors onto the partitions, 4 bytes each"):
                sp.dma_start(lnw[:], column(ln_w)).then_inc(consts_in, 16)
                sp.dma_start(g_c[:], column(g_in)).then_inc(consts_in, 16)
                sp.dma_start(b_c[:], column(b_in)).then_inc(consts_in, 16)
                sp.dma_start(b1_c[:], column(b1)).then_inc(consts_in, 16)
                sp.dma_start(bd1_c[:], column(bd1)).then_inc(consts_in, 16)
            sp.dma_start(b2_b[:], spread(b2)).then_inc(consts_in, 16)
            sp.dma_start(w_all[:, :, 0:F], w_root.rearrange("(k p) f -> p k f", p=128)).then_inc(w_in, 16)
            for r in range(R):
                sp.dma_start(w_all[:, :, (r + 1) * F:(r + 2) * F],
                             w_rel[r].rearrange("(k p) f -> p k f", p=128)).then_inc(w_in, 16)
            with sp.Fori(1, T) as t:
                sp.wait_ge(xn_ready, t)
                sp.dma_start(xt[:], x_t[bass.ds(t, 1)].rearrange("o p d -> (o p) d")).then_inc(x_in, 16)
            sp.wait_ge(xn_ready, T)
            sp.dma_start(xt[:], x_t[0]).then_inc(x_in, 16)
            sp.wait_ge(adj_done, 1)
            sp.wait_ge(proj_mm, 1 + 2 * T)
            sp.dma_start(wo_s[:, 0:2, :], wo[0:256].rearrange("(k p) d -> p k d", p=128)).then_inc(wo_in, 16)
            sp.dma_start(wo_s[0:FB[2], 2, :], wo[256:F]).then_inc(wo_in, 16)
            sp.dma_start(cb_b[:], spread(conv_b)).then_inc(wo_in, 16)
            sp.dma_start(x_last[:], x_t[T - 1]).then_inc(wo_in, 16)
            with sp.Fori(1, T - 1) as t:
                sp.wait_ge(res_done, t)
                sp.dma_start(xt[:], x_t[bass.ds(t, 1)].rearrange("o p d -> (o p) d")).then_inc(x_in, 16)
            sp.wait_ge(agg_mm, T)
            sp.wait_ge(adj_sum, T)
            for f in range(K1):
                cols = slice(f * 128, (f + 1) * 128)
                sp.dma_start(w1_s[:, :, cols], w1[:, cols].rearrange("(k p) f -> p k f", p=128)).then_inc(w1_in[f], 16)
            sp.dma_start(w2_s[:], w2.rearrange("(k p) f -> p k f", p=128)).then_inc(w2_in, 16)
            sp.wait_ge(rel0_added, T)
            for a, d in ((bb_b, bb), (ng_b, ng), (nb_b, nb)):
                sp.dma_start(a[:], d.rearrange("l d -> (l d)").rearrange("(o d) -> o d", o=1)
                             .broadcast_to([P, L * HB]).rearrange("p (l d) -> p l d", l=L)).then_inc(rows_in, 16)
            for i in range(L):
                if i > 0:
                    sp.wait_ge(wb_mm, T * i)
                sp.dma_start(wa_s[:], wa[i].rearrange("(k p) f -> p k f", p=128)).then_inc(wab_in, 16)
                sp.dma_start(wb_s[:], wb[i].rearrange("(k p) f -> p k f", p=128)).then_inc(wab_in, 16)
                with nc.allow_non_contiguous_dma(reason="a vector onto the partitions, 4 bytes each"):
                    sp.dma_start(ba_c[:], column(ba[i])).then_inc(wab_in, 16)
                if i == 0:
                    sp.wait_ge(h_mm, 1 + T)
                    sp.dma_start(wd1_s[:], wd1.rearrange("(k p) f -> p k f", p=128)).then_inc(wd_in, 16)
                    sp.dma_start(wd2_s[:], wd2.rearrange("(k p) f -> p k f", p=128)).then_inc(wd_in, 16)
                    for a, d in ((bd2_b, bd2), (go_b, g_out), (bo_b, b_out)):
                        sp.dma_start(a[:], spread(d)).then_inc(wd_in, 16)
            with sp.Fori(0, T // 2) as c:
                for u in range(2):
                    sp.wait_ge(f_done, 1 + c * 2 + u + 1)
                    sp.dma_start(out_t[bass.ds(c * 2 + u, 1)].rearrange("o p d -> (o p) d"),
                                 ot[:, u]).then_inc(out_done, 16)
            sp.wait_ge(out_done, 16 + 16 * T)

        @block.gpsimd
        def _(pool):
            pool.iota(iota_r[:], [[1, 128]], base=0, channel_multiplier=0,
                      allow_small_or_imprecise_dtypes=True).then_inc(iotas, 1)
            pool.iota(iota_i[:], [[0, 1]], base=0, channel_multiplier=1,
                      allow_small_or_imprecise_dtypes=True).then_inc(iotas, 1)
            pool.iota(iota_l[:], [[1, P]], base=0, channel_multiplier=0,
                      allow_small_or_imprecise_dtypes=True).then_inc(iotas, 1)
            pool.iota(iota_c[:], [[1, R * C]], base=0, channel_multiplier=0,
                      allow_small_or_imprecise_dtypes=True).then_inc(iotas, 1)
            pool.memset(adj[:, 0], 0.0).then_inc(adj_zero, 1)
            pool.wait_ge(adj_sum, T)
            for t in range(T):
                pool.wait_ge(ln2_shift, t + 1)
                if t >= 2:
                    pool.wait_ge(xhT_ps, 2 * t - 2)
                pool.tensor_scalar(xh[:, t % 2], x1[:, t], small2[:, 2, t:t + 1], small2[:, 3, t:t + 1],
                                   ALU.mult, ALU.add).then_inc(xh_ready, 1)
            def low_part(t, made):
                pool.wait_ge(hi_done, made)
                pool.tensor_tensor(h_lo[:, t], h[:, t], h_hi[:, t], ALU.subtract).then_inc(lo_done, 1)

            for t in range(T):
                low_part(t, t + 1)
            with pool.Fori(1, L) as i:
                for t in range(T):
                    low_part(t, i * T + t + 1)

            pool.wait_ge(wd_in, 80)
            pool.wait_ge(wa_mm, L * 2 * len(CH))
            for c in range(T // 2):
                a = x1[:, 2 * c:2 * c + 2]
                pool.wait_ge(o_sum, 1 + c * 2)
                for u in range(2):
                    ins = pool.tensor_tensor(x_bd[:, u], a[:, u], bd2_b[:], ALU.add)
                ins.then_inc(xb_done, 1)
                pool.wait_ge(o_res, 1 + c)
                for u in range(2):
                    ins = pool.tensor_tensor(x_bo[:, u], a[:, u], bo_b[:], ALU.add)
                ins.then_inc(xo_done, 1)

        @block.scalar
        def _(act):
            for s in (xnT_copied, y_copied, hT_lo, r1_done, d1_done,):
                act.sem_inc(s, 1)
            act.wait_ge(small_set, 4)
            act.activation(adj[:, 1].rearrange("p b d -> p (b d)"),
                           zero[:, 0:1].broadcast_to([P, T * ND]), ACT.Copy).then_inc(adj_zero, 1)

            def root_norm(t):
                act.wait_ge(x_in, (t + 1) * 16)
                act.activation(xn[:], xt[:], ACT.Square, accum_out=small1[:, 0:1]).then_inc(xn_sq, 1)
                act.wait_ge(xn_sq, t + 1)
                act.activation(small1[:, 1:2], small1[:, 0:1], ACT.Sqrt, bias=eps0[:, 0:1],
                               scale=1.0 / D).then_inc(xn_sd, 1)
                act.wait_ge(xn_rstd, t + 1)
                act.activation(xn[:], xt[:], ACT.Copy, scale=small1[:, 2:3]).then_inc(xn_ready, 1)

            def weigh(q):
                for i in range(4):
                    k = 4 * q + i
                    ins = act.activation(xnT[:, k], pb[:, 7, i * P:(i + 1) * P], ACT.Copy,
                                         scale=lnw[:, k:k + 1])
                ins.then_inc(xnT_copied, 1)

            def tile_of_1(t, last):
                act.wait_ge(xnT_ps, t * 2 + 2)
                act.wait_ge(proj_mm, 1 + t * 2)
                weigh(1)
                if not last:
                    root_norm(t + 1)
                    act.wait_ge(xnT_ps, t * 2 + 3)
                    act.wait_ge(proj_mm, 1 + t * 2 + 1)
                    weigh(0)
                wait_apart(act, proj_mm, 1 + t * 2 + 2)
                yt = y[:, bass.ds(t, 1)].rearrange("p o f -> p (o f)")
                act.copy(yt[:, 0:F], pb[0:P, 4, 0:F])
                act.copy(yt[:, F:2 * F], pb[0:P, 5, 0:F])
                act.copy(yt[:, 2 * F + 1:3 * F + 1], pb[0:P, 6, 0:F]).then_inc(y_copied, 1)

            act.wait_ge(consts_in, 16 * 6)
            root_norm(0)
            act.wait_ge(xnT_ps, 1)
            weigh(0)
            act.wait_ge(codes_ready, 1)
            with act.Fori(0, T - 1) as t:
                tile_of_1(t, False)
            tile_of_1(T - 1, True)

            def elu_parts_of(t):
                act.wait_ge(neg_part, t + 1)
                act.activation(ybuf[:, 2], ybuf[:, 1], ACT.Exp)
                act.activation(ybuf[:, 3], ybuf[:, 0], ACT.Relu).then_inc(elu_parts, 1)

            def turned(t):
                act.wait_ge(yT_ps, t + 1)
                act.wait_ge(wo_mm, 1 + t)
                act.copy(yT[:, 0:2].rearrange("p k n -> p (k n)"), pb[:, 4, 0:2 * P])
                act.copy(yT[0:FB[2], 2], pb[0:FB[2], 4, 2 * P:3 * P]).then_inc(yT_copied, 1)

            def first_norm(t):
                act.wait_ge(res_mv, t + 1)
                act.activation(small2[:, 0, t:t + 1], mv[:, t, 1:2], ACT.Sqrt, bias=epsc[:, 0:1]).then_inc(ln1_sd, 1)
                act.wait_ge(ln1_shift, t + 1)
                act.activation(x1[:, t], x1[:, t], ACT.Identity, scale=small2[:, 0, t:t + 1],
                               bias=small2[:, 1, t:t + 1]).then_inc(x1_ready, 1)

            def second_sd(t):
                act.wait_ge(x1_mv, t + 1)
                act.activation(small2[:, 2, t:t + 1], mv[:, t, 3:4], ACT.Sqrt, bias=epsc[:, 0:1]).then_inc(ln2_sd, 1)

            def weigh_first(c):
                act.wait_ge(r1_mm, 1 + c * K1)
                act.wait_ge(xhT_ps, c * 4 + 1)
                for i in range(4):
                    ins = act.activation(hT[:, i, 0:P], pb[:, 0, i * P:(i + 1) * P], ACT.Identity,
                                         scale=g_c[:, i:i + 1], bias=b_c[:, i:i + 1])
                ins.then_inc(hT_lo, 1)

            def relus_of_3(c, blocks):
                for f in blocks:
                    if f == 0:
                        act.wait_ge(h_mm, 1 + c * 2)
                    act.wait_ge(r1_mm, 1 + c * K1 + f + 1)
                    act.activation(r1T[:, f], pb[:, 4 + f % 2, 0:2 * P],
                                   ACT.Relu, bias=b1_c[:, f:f + 1]).then_inc(r1_done, 1)

            elu_parts_of(0)
            for t in range(1, T):
                turned(t - 1)
                elu_parts_of(t)
                if t < T - 1:
                    first_norm(t - 1)
                    second_sd(t - 1)
            act.wait_ge(adj_sum, T)
            weigh_first(0)
            turned(T - 1)
            for f in range(2):
                relus_of_3(0, [f])
                first_norm(T - 2 + f)
                second_sd(T - 2 + f)
            relus_of_3(0, range(2, K1))
            with act.Fori(1, T // 2) as c:
                weigh_first(c)
                relus_of_3(c, range(K1))

            def high_part(t, made):
                act.wait_ge(h_done, 1 + made)
                act.copy(h_hi[:, t], h[:, t]).then_inc(hi_done, 1)

            act.wait_ge(h_mm, 1 + T)
            for t in range(T):
                high_part(t, t + 1)

            def layer(i, last):
                act.wait_ge(z_mm, i + 1)
                for c, (c0, n) in enumerate(CH):
                    act.copy(zT[:, 0, c0:c0 + n], pb[:, c, 0:n]).then_inc(z_lo, 1)
                for c, (c0, n) in enumerate(CH):
                    act.wait_ge(wa_mm, i * 6 + 2 * c + 1)
                    act.activation(rT[:, 0, c0:c0 + n], pb[:, c, 0:n], ACT.Relu,
                                   bias=ba_c[:, 0:1]).then_inc(r_lo, 1)
                for t in range(T):
                    act.wait_ge(z_mv, i * T + t + 1)
                    act.activation(small4[:, 2 + t % 2:3 + t % 2], mv4[:, t % 2, 1:2], ACT.Sqrt,
                                   bias=epsc[:, 0:1]).then_inc(z_sd, 1)
                    if t > 0 and not last:
                        high_part(t - 1, (i + 1) * T + t)
                if not last:
                    high_part(T - 1, (i + 1) * T + T)

            with act.Fori(0, L - 1) as i:
                layer(i, False)
            layer(L - 1, True)

            def copies(c):
                act.wait_ge(h3T_ps, c + 1)
                act.wait_ge(d1_mm, 1 + c * K1)
                act.copy(h3T[:].rearrange("p k (u n) -> p u k n", u=2),
                         pb[:, 0, 0:4 * P].rearrange("p (u k n) -> p u k n", u=2, k=K2)).then_inc(h3T_done, 1)

            def relus(c, blocks):
                for f in blocks:
                    if f == 0:
                        act.wait_ge(d2_mm, 1 + c * 2)
                    act.wait_ge(d1_mm, 1 + c * K1 + f + 1)
                    act.activation(dT[:, f], pb[:, 1 + f % 2, 0:2 * P], ACT.Relu,
                                   bias=bd1_c[:, f:f + 1]).then_inc(d1_done, 1)

            def deviation(c, k, s_mv, m, s_sd):
                act.wait_ge(s_mv, c + 1)
                act.activation(sd5[:, k], m[:, :, 1], ACT.Sqrt, bias=epsc[:, 0:1]).then_inc(s_sd, 1)

            copies(0)
            relus(0, range(K1))
            with act.Fori(0, T // 2 - 1) as c:
                copies(c + 1)
                relus(c + 1, range(2))
                deviation(c, 0, o_mv, mv4, o_sd)
                relus(c + 1, range(2, K1))
                deviation(c, 1, f_mv, mv5, f_sd)
            deviation(T // 2 - 1, 0, o_mv, mv4, o_sd)
            deviation(T // 2 - 1, 1, f_mv, mv5, f_sd)

        @block.tensor
        def _(pe):
            for s in (proj_mm, wo_mm, r1_mm, h_mm, d1_mm, d2_mm,):
                pe.sem_inc(s, 1)
            pe.wait_ge(small_set, 5)
            pe.wait_ge(edges_ready, 1)
            for f, a in enumerate((e_low, e_code, e_base, e_far)):
                for j in range(J):
                    pe.transpose(pb[0:P, f, j * G:(j + 1) * G], a[:, j * P:(j + 1) * P], ident[0:G, 0:G])
            for i in range(2):
                ins = pe.transpose(pb[0:1, 4, i * 128:i * 128 + G], gmin[:, i:i + 1], ident[0:G, 0:G])
            ins.then_inc(edges_ps, 1)

            def count(b):
                for j in range(J):
                    ins = pe.matmul(pb[0:P, b, 0:R * C], oh_low[:, b, j], oh_code[:, b, j],
                                    start=(j == 0), stop=(j == J - 1))
                return ins

            def turn(q):
                for i in range(4):
                    k = 4 * q + i
                    ins = pe.transpose(pb[:, 7, i * P:(i + 1) * P], xn[:, k * 128:(k + 1) * 128], ident[0:P, 0:P])
                ins.then_inc(xnT_ps, 1)

            def tile_of_1(t, last):
                for u in range(UG):
                    pe.wait_ge(onehots, t * UG + u + 1)
                    pe.wait_ge(counts_free, t * UG + u + 1)
                    count(u % 2).then_inc(counts_mm, 1)
                    if u == 0:
                        pe.wait_ge(xnT_copied, 1 + t * 2 + 1)
                        turn(1)
                        pe.wait_ge(y_copied, 1 + t)
                    if u == 4:
                        pe.wait_ge(xnT_copied, 1 + t * 2 + 2)
                        if not last:
                            pe.wait_ge(xn_ready, t + 2)
                            turn(0)
                    for n in range(3):
                        ins = pe.matmul(pb[0:P, 4 + n, 0:F], xnT[:, u], w_all[:, u, n * F:(n + 1) * F],
                                        start=(u == 0), stop=(u == KD - 1))
                    if u in (3, KD - 1):
                        ins.then_inc(proj_mm, 1)

            pe.wait_ge(xn_ready, 1)
            turn(0)
            pe.wait_ge(codes_ready, 1)
            pe.wait_ge(w_in, 48)
            with pe.Fori(0, T - 1) as t:
                tile_of_1(t, False)
            tile_of_1(T - 1, True)

            far = pe.value_load(seln[0:1, 0:1], min_val=0, max_val=1)
            with pe.If(far > 0):
                with pe.Fori(0, NW * G) as i:
                    pe.wait_ge(s_onehots, i + 1)
                    count(0).then_inc(s_counts_mm, 1)

            def project(t):
                pe.wait_ge(elu_done, t + 1)
                f0 = 0
                for i, n in enumerate(FB):
                    ins = pe.transpose(pb[0:n, 4, i * P:(i + 1) * P], ybuf[:, 4, f0:f0 + n], ident[0:P, 0:P])
                    f0 += n
                ins.then_inc(yT_ps, 1)
                pe.wait_ge(yT_copied, t + 1)
                if t > 0:
                    pe.wait_ge(res_done, t)
                for q in range(2):
                    for i, n in enumerate(FB):
                        ins = pe.matmul(pb[0:P, 5 + q], yT[0:n, i], wo_s[0:n, i, q * 512:(q + 1) * 512],
                                        start=(i == 0), stop=(i == 2))
                ins.then_inc(wo_mm, 1)

            def turn_chunk(c):
                for u in range(2):
                    pe.wait_ge(xh_ready, c * 2 + u + 1)
                    for q in range(2):
                        for i in range(4):
                            k = 4 * q + i
                            ins = pe.transpose(pb[:, 2 * u + q, i * P:(i + 1) * P],
                                               xh[:, u, k * 128:(k + 1) * 128], ident[0:P, 0:P])
                        ins.then_inc(xhT_ps, 1)

            def chunk_of_3(c, last):
                pe.wait_ge(hT_lo, 1 + c + 1)
                pe.wait_ge(hT_hi, 1 + c + 1)
                pe.wait_ge(r1_done, 1 + c * K1)
                for f in range(K1):
                    if f == 1:
                        pe.wait_ge(res_done, T)
                    if f >= 2:
                        pe.wait_ge(r1_done, 1 + c * K1 + f - 1)
                    pe.wait_ge(w1_in[f], 16)
                    for k in range(KD):
                        ins = pe.matmul(pb[:, 4 + f % 2, 0:2 * P], w1_s[:, k, f * 128:(f + 1) * 128], hT[:, k],
                                        start=(k == 0), stop=(k == KD - 1))
                    ins.then_inc(r1_mm, 1)
                if not last:
                    turn_chunk(c + 1)
                pe.wait_ge(r1_done, 1 + c * K1 + K1)
                pe.wait_ge(w2_in, 16)
                pe.wait_ge(h_done, 1 + c * 2)
                for u in range(2):
                    for k in range(K1):
                        ins = pe.matmul(pb[0:P, 6 + u, 0:HB], r1T[:, k, u * P:(u + 1) * P], w2_s[:, k],
                                        start=(k == 0), stop=(k == K1 - 1))
                    ins.then_inc(h_mm, 1)

            pe.wait_ge(adj_done, 1)
            pe.wait_ge(y_copied, 1 + T)
            for t in range(T):
                if t >= 2:
                    pe.wait_ge(pre_elu, t - 1)
                for s in range(T):
                    for r in range(R):
                        ins = pe.matmul(pb[0:P, 2 * (t % 2) + r, 0:F + 1], adj[:, r, s, t * P:(t + 1) * P],
                                        y[:, s, F + r * (F + 1):F + (r + 1) * (F + 1)],
                                        start=(s == 0), stop=(s == T - 1))
                ins.then_inc(agg_mm, 1)
                if t == 1:
                    pe.wait_ge(wo_in, 64)
                if t > 0:
                    project(t - 1)
            pe.wait_ge(pre_elu, T)
            turn_chunk(0)
            pe.wait_ge(deg_set, 1)
            pe.transpose(pb[0:1, 7, 0:P], degmax[:, 0:1], ident[0:P, 0:P]).then_inc(deg_ps, 1)
            project(T - 1)

            pe.wait_ge(deg_set, 2)
            with pe.Fori(0, T // 2 - 1) as c:
                chunk_of_3(c, False)
            chunk_of_3(T // 2 - 1, True)

            pe.wait_ge(big_ready, 1)
            big = pe.value_load(bign[0:1, 0:1], min_val=0, max_val=1)

            def aggregate(s):
                with pe.If(big > 0):
                    for f in range(K2):
                        for c, (c0, n) in enumerate(CH):
                            ins = pe.matmul(pb[:, 3 * f + c, 0:n], h[:, s, f * 128:(f + 1) * 128],
                                            adj[:, 0, s, c0:c0 + n], start=(s == 0), stop=(s == T - 1))
                    if s == T - 1:
                        ins.then_inc(z_mm, 1)
                with pe.Else():
                    for f in range(K2):
                        for part in (h_hi, h_lo):
                            for c, (c0, n) in enumerate(CH):
                                ins = pe.matmul(pb[:, 3 * f + c, 0:n], part[:, s, f * 128:(f + 1) * 128],
                                                adj_r[:, s, c0:c0 + n], start=(s == 0 and part is h_hi),
                                                stop=(s == T - 1 and part is h_lo))
                    if s == T - 1:
                        ins.then_inc(z_mm, 1)

            def layer(i, last):
                pe.wait_ge(wab_in, i * 48 + 48)
                for c, (c0, n) in enumerate(CH):
                    pe.wait_ge(z_lo, i * 3 + c + 1)
                    pe.wait_ge(z_hi, i * 3 + c + 1)
                    for f in range(K2):
                        for k in range(K2):
                            ins = pe.matmul(pb[:, 3 * f + c, 0:n], wa_s[:, k, f * 128:(f + 1) * 128],
                                            zT[:, k, c0:c0 + n], start=(k == 0), stop=(k == K2 - 1))
                        ins.then_inc(wa_mm, 1)

                def second(t):
                    c = [c for c, (c0, n) in enumerate(CH) if c0 <= t * P < c0 + n][0]
                    pe.wait_ge(r_lo, i * 3 + c + 1)
                    pe.wait_ge(r_hi, i * 3 + c + 1)
                    pe.wait_ge(z_b, 1 + i * T + max(t - 1, 0))
                    for k in range(K2):
                        ins = pe.matmul(pb[0:P, 6 + t % 2, 0:HB], rT[:, k, t * P:(t + 1) * P], wb_s[:, k],
                                        start=(k == 0), stop=(k == K2 - 1))
                    ins.then_inc(wb_mm, 1)

                for t in range(T + LAG if not last else T):
                    if t < T:
                        second(t)
                    if t >= LAG and not last:
                        if t == LAG:
                            pe.wait_ge(r_lo, i * 3 + 3)
                            pe.wait_ge(r_hi, i * 3 + 3)
                        pe.wait_ge(lo_done, (i + 1) * T + t - LAG + 1)
                        aggregate(t - LAG)

            pe.wait_ge(adj_exact, 1)
            for s in range(T):
                pe.wait_ge(lo_done, s + 1)
                aggregate(s)
            with pe.Fori(0, L - 1) as i:
                layer(i, False)
            layer(L - 1, True)

            def turn_h(c):
                pe.wait_ge(h_done, 1 + L * T + 2 * c + 2)
                if c == 0:
                    pe.wait_ge(r_lo, 3 * L)
                    pe.wait_ge(r_hi, 3 * L)
                else:
                    pe.wait_ge(h3T_done, c)
                for u in range(2):
                    for k in range(K2):
                        ins = pe.transpose(pb[:, 0, (2 * u + k) * P:(2 * u + k + 1) * P],
                                           h[:, 2 * c + u, k * 128:(k + 1) * 128], ident[0:P, 0:P])
                ins.then_inc(h3T_ps, 1)

            turn_h(0)
            pe.wait_ge(wd_in, 80)
            for c in range(T // 2):
                pe.wait_ge(h3T_done, c + 1)
                pe.wait_ge(d1_done, 1 + c * K1)
                for f in range(K1):
                    if f >= 2:
                        pe.wait_ge(d1_done, 1 + c * K1 + f - 1)
                    for k in range(K2):
                        ins = pe.matmul(pb[:, 1 + f % 2, 0:2 * P],
                                        wd1_s[:, k, f * 128:(f + 1) * 128], h3T[:, k],
                                        start=(k == 0), stop=(k == K2 - 1))
                    ins.then_inc(d1_mm, 1)
                if c + 1 < T // 2:
                    turn_h(c + 1)
                pe.wait_ge(d1_done, 1 + c * K1 + K1)
                for u in range(2):
                    pe.wait_ge(o_sum, 1 + max(c * 2 + u - 1, 0))
                    if c == 0 and u == 1:
                        pe.wait_ge(z_b, 1 + L * T)
                    for q in range(2):
                        for k in range(K1):
                            ins = pe.matmul(pb[0:P, 3 + 2 * u + q], dT[:, k, u * P:(u + 1) * P],
                                            wd2_s[:, k, q * 512:(q + 1) * 512],
                                            start=(k == 0), stop=(k == K1 - 1))
                    ins.then_inc(d2_mm, 1)

        @block.vector
        def _(dve):
            for s in (hT_hi, h_done, z_b, o_sum, o_res, f_done):
                dve.sem_inc(s, 1)
            dve.memset(eps0[:], EPS0).then_inc(small_set, 1)
            dve.memset(epsc[:], EPS).then_inc(small_set, 1)
            dve.memset(zero[:], 0.0).then_inc(small_set, 1)
            dve.memset(mini[:], 0).then_inc(small_set, 1)
            dve.wait_ge(iotas, 4)
            dve.tensor_scalar(ident[:], iota_r[:], iota_i[:, 0:1], None, ALU.is_equal).then_inc(small_set, 1)

            steps = [0]

            def step(ins):
                ins.then_inc(prep, 1)
                steps[0] += 1
                dve.wait_ge(prep, steps[0])

            dve.wait_ge(edges_in, 48)
            dve.tensor_copy(e_low[:], src_i[:])
            dve.tensor_copy(e_base[:], typ_i[:])
            step(dve.tensor_copy(e_far[:], dst_i[:]))
            step(dve.tensor_reduce(gmin[:, 0:1], e_far[:], AX.X, ALU.min))
            dve.tensor_scalar(e_rel[:], e_far[:], gmin[:, 0:1], None, ALU.subtract)
            step(dve.tensor_scalar(e_blk[:], e_low[:], -float(P // 2), 1.0 / P, ALU.add, ALU.mult))
            step(dve.tensor_scalar(e_blk[:], e_blk[:], ROUND, None, ALU.add))
            step(dve.tensor_scalar(e_blk[:], e_blk[:], -ROUND, None, ALU.add))
            dve.scalar_tensor_tensor(e_low[:], e_blk[:], -float(P), e_low[:], ALU.mult, ALU.add)
            step(dve.tensor_scalar(e_base[:], e_base[:], float(C), None, ALU.mult))
            step(dve.scalar_tensor_tensor(e_base[:], e_blk[:], float(W), e_base[:], ALU.mult, ALU.add))
            step(dve.tensor_scalar(e_blk[:], e_rel[:], float(W), None, ALU.is_ge))
            dve.tensor_reduce(gmin[:, 1:2], e_blk[:], AX.X, ALU.max)
            dve.scalar_tensor_tensor(e_far[:], e_blk[:], -float(FAR), e_far[:], ALU.mult, ALU.add)
            step(dve.scalar_tensor_tensor(e_rel[:], e_blk[:], float(FAR), e_rel[:], ALU.mult, ALU.add))
            dve.tensor_scalar(e_far[:], e_far[:], float(FAR), None, ALU.add)
            dve.tensor_tensor(e_code[:], e_rel[:], e_base[:], ALU.add).then_inc(edges_ready, 1)
            dve.wait_ge(xn_sd, 1)
            dve.reciprocal(small1[:, 2:3], small1[:, 1:2]).then_inc(xn_rstd, 1)
            dve.memset(edgeT[:], 0.0).then_inc(prep, 1)
            steps[0] += 1
            dve.wait_ge(prep, steps[0])
            dve.wait_ge(edges_ps, 1)
            for f in range(4):
                dve.tensor_copy(edgeT[:, f, :, 0:G], pb[0:P, f, 0:J * G].rearrange("p (j g) -> p j g", j=J))
            dve.tensor_copy(mini[0:1, 0:G], pb[0:1, 4, 0:G])
            dve.memset(y[:, :, 2 * F:2 * F + 1], 1.0)
            dve.memset(y[:, :, 3 * F + 1:3 * F + 2], 1.0)
            step(dve.tensor_reduce(small1[0:1, 4:5], pb[0:1, 4, 128:128 + G], AX.X, ALU.max))
            dve.tensor_copy(seln[0:1, 0:1], small1[0:1, 4:5]).then_inc(codes_ready, 1)
            for _i in range(2):
                dve.memset(small1[:, 5 + _i:6 + _i], 0.0).then_inc(counts_free, 1)
            dve.wait_ge(codes_ready, 1)

            def build(g, b, low, code):
                for j in range(J):
                    dve.tensor_scalar(oh_low[:, b, j], iota_l[:], low(j, g), None, ALU.is_equal)
                for j in range(J):
                    ins = dve.tensor_scalar(oh_code[:, b, j], iota_c[:], code(j, g), None, ALU.is_equal)
                return ins

            def low_of(j, g):
                return edgeT[:, 0, j, bass.ds(g, 1)]

            def code_of(j, g):
                return edgeT[:, 1, j, bass.ds(g, 1)]

            for g in range(2):
                build(g, g, low_of, code_of).then_inc(onehots, 1)
            dve.wait_ge(adj_zero, 2)

            def tile_of_1(t, last):
                base = nc.values_load_multi_w_load_instructions(
                    mini[0:1, bass.ds(t * UG, UG)], engines=[mybir.EngineType.DVE], min_val=0, max_val=N - 1)[1]
                for u in range(UG):
                    if u == 2 and not last:
                        dve.wait_ge(xn_sd, t + 2)
                        dve.reciprocal(small1[:, 2:3], small1[:, 1:2]).then_inc(xn_rstd, 1)
                    g = t * UG + u
                    dve.wait_ge(counts_mm, g + 1)
                    dve.wait_ge(counts_free, g + 2)
                    place = adj[:, :, :, bass.ds(base[u], W)]
                    dve.tensor_tensor(place, place, window(u % 2), ALU.add).then_inc(counts_free, 1)
                    build(g + 2, u % 2, low_of, code_of).then_inc(onehots, 1)

            with dve.Fori(0, T - 1) as t:
                tile_of_1(t, False)
            tile_of_1(T - 1, True)

            dve.wait_ge(counts_free, G + 2)
            dve.wait_ge(onehots, G + 2)
            far = dve.value_load(seln[0:1, 0:1], min_val=0, max_val=1)
            with dve.If(far > 0):
                dist = edgeT[:, 3]
                with dve.Fori(0, NW) as w:
                    dve.tensor_scalar(maskS[:, 0], dist, 0.0, float(FAR), ALU.is_lt, ALU.mult)
                    dve.tensor_scalar(maskS[:, 1], dist, float(W), float(FAR), ALU.is_ge, ALU.mult)
                    dve.tensor_tensor(codeS[:], dist, edgeT[:, 2], ALU.add).then_inc(s_codes, 1)
                    dve.wait_ge(s_codes, w * 4 + 1)
                    dve.tensor_tensor(codeS[:], codeS[:], maskS[:, 0], ALU.add).then_inc(s_codes, 1)
                    dve.wait_ge(s_codes, w * 4 + 2)
                    dve.tensor_tensor(codeS[:], codeS[:], maskS[:, 1], ALU.add).then_inc(s_codes, 1)
                    dve.tensor_scalar(dist, dist, -float(W), None, ALU.add).then_inc(s_codes, 1)
                    with dve.Fori(0, G) as g:
                        dve.wait_ge(s_codes, w * 4 + 4)
                        build(g, 0, low_of, lambda j, g: codeS[:, j, bass.ds(g, 1)]).then_inc(s_onehots, 1)
                        dve.wait_ge(s_counts_mm, w * G + g + 1)
                        place = adj[:, :, :, bass.ds(w * W, W)]
                        dve.tensor_tensor(place, place, window(0), ALU.add).then_inc(s_added, 1)
                        dve.wait_ge(s_added, w * G + g + 1)
            dve.memset(small1[:, 7:8], 0.0).then_inc(adj_done, 1)

            dve.wait_ge(wo_in, 64)
            dve.wait_ge(y_copied, 1 + T)
            sums, below, exps, above, elu = (ybuf[:, i] for i in range(5))

            def relations(t, b):
                dve.tensor_tensor(sums, y[:, t, 0:F], cb_b[:], ALU.add).then_inc(root_b, 1)
                dve.wait_ge(agg_mm, t + 1)
                dve.tensor_scalar(rc[:, :, 0:1], pb[0:P, 2 * b:2 * b + 2, F:F + 1], 1.0, None, ALU.max).then_inc(cnt_max, 1)
                dve.wait_ge(cnt_max, t + 1)
                dve.reciprocal(rc[:, :, 1:2], rc[:, :, 0:1]).then_inc(cnt_rcp, 1)
                dve.tensor_tensor(deg[:, t:t + 1], pb[0:P, 2 * b, F:F + 1], rc[:, 1, 0:1], ALU.add).then_inc(deg_sum, 1)
                dve.wait_ge(cnt_rcp, t + 1)
                dve.wait_ge(root_b, t + 1)
                dve.scalar_tensor_tensor(sums, pb[0:P, 2 * b, 0:F], rc[:, 0, 1:2], sums, ALU.mult, ALU.add).then_inc(rel0_added, 1)
                dve.wait_ge(rel0_added, t + 1)
                dve.scalar_tensor_tensor(sums, pb[0:P, 2 * b + 1, 0:F], rc[:, 1, 1:2], sums, ALU.mult, ALU.add).then_inc(pre_elu, 1)
                dve.wait_ge(pre_elu, t + 1)
                dve.tensor_scalar(below, sums, 0.0, None, ALU.min).then_inc(neg_part, 1)
                cols = slice(t * P, (t + 1) * P)
                dve.tensor_tensor(adj[:, 0, :, cols], adj[:, 0, :, cols], adj[:, 1, :, cols], ALU.add).then_inc(adj_sum, 1)
                dve.wait_ge(elu_parts, t + 1)
                if t > 0:
                    dve.wait_ge(yT_ps, t)
                dve.scalar_tensor_tensor(elu, exps, -1.0, above, ALU.add, ALU.add).then_inc(elu_done, 1)
                dve.wait_ge(adj_sum, t + 1)
                dve.tensor_tensor(adj[:, 0, t, cols], adj[:, 0, t, cols], ident[0:P, 0:P], ALU.add).then_inc(adj_self, 1)

            def residual(t):
                dve.wait_ge(wo_mm, 1 + t + 1)
                if t < T - 1:
                    dve.wait_ge(x_in, 16 * (T + t + 1))
                dve.scalar_tensor_tensor(x1[:, t], xt[:] if t < T - 1 else x_last[:], 2.0, pb[0:P, 5:7].rearrange("p a b -> p (a b)"),
                                         ALU.mult, ALU.add).then_inc(res_done, 1)
                dve.wait_ge(res_done, t + 1)
                dve.bn_stats(st2[:, 0], x1[:, t, 0:512])
                dve.bn_stats(st2[:, 1], x1[:, t, 512:D]).then_inc(res_stats, 1)
                dve.wait_ge(res_stats, t + 1)
                dve.bn_aggr(mv[:, t, 0:2], st2[:].rearrange("p a b -> p (a b)")).then_inc(res_mv, 1)
                dve.wait_ge(res_mv, t + 1)

            def shift(t, m, r, sd, rstd, done):
                dve.wait_ge(sd, t + 1)
                dve.reciprocal(small2[:, r, t:t + 1], small2[:, r, t:t + 1]).then_inc(rstd, 1)
                dve.wait_ge(rstd, t + 1)
                dve.scalar_tensor_tensor(small2[:, r + 1, t:t + 1], mv[:, t, m:m + 1], -1.0, small2[:, r, t:t + 1],
                                         ALU.mult, ALU.mult).then_inc(done, 1)

            def norms(t):
                shift(t, 0, 0, ln1_sd, ln1_rstd, ln1_shift)
                dve.wait_ge(x1_ready, t + 1)
                dve.bn_stats(st2[:, 0], x1[:, t, 0:512])
                dve.bn_stats(st2[:, 1], x1[:, t, 512:D]).then_inc(x1_stats, 1)
                dve.wait_ge(x1_stats, t + 1)
                dve.bn_aggr(mv[:, t, 2:4], st2[:].rearrange("p a b -> p (a b)")).then_inc(x1_mv, 1)
                dve.wait_ge(x1_mv, t + 1)
                shift(t, 2, 2, ln2_sd, ln2_rstd, ln2_shift)

            def weigh_turned(c):
                dve.wait_ge(r1_mm, 1 + c * K1)
                for u, q in ((0, 1), (1, 0), (1, 1)):
                    dve.wait_ge(xhT_ps, c * 4 + 2 * u + q + 1)
                    for i in range(4):
                        k = 4 * q + i
                        ins = dve.tensor_scalar(hT[:, k, u * P:(u + 1) * P], pb[:, 2 * u + q, i * P:(i + 1) * P],
                                                g_c[:, k:k + 1], b_c[:, k:k + 1], ALU.mult, ALU.add)
                ins.then_inc(hT_hi, 1)

            def first_h(c):
                for u in range(2):
                    dve.wait_ge(h_mm, 1 + c * 2 + u + 1)
                    dve.tensor_tensor(h[:, bass.ds(c * 2 + u, 1)].rearrange("p o d -> p (o d)"),
                                      pb[0:P, 6 + u, 0:HB], b2_b[:], ALU.add).then_inc(h_done, 1)

            for t in range(T):
                relations(t, t % 2)
                if t == T - 1:
                    dve.wait_ge(deg_sum, T)
                    dve.tensor_reduce(degmax[:, 0:1], deg[:], AX.X, ALU.max).then_inc(deg_set, 1)
                if t > 0:
                    residual(t - 1)
                    if t < T - 1:
                        norms(t - 1)

            weigh_turned(0)
            dve.wait_ge(deg_ps, 1)
            dve.tensor_reduce(degmax[0:1, 1:2], pb[0:1, 7, 0:P], AX.X, ALU.max).then_inc(deg_set, 1)
            residual(T - 1)
            for t in (T - 2, T - 1):
                norms(t)
            dve.wait_ge(deg_set, 2)
            dve.tensor_scalar(bign[0:1, 0:1], degmax[0:1, 1:2], float(EXACT), None, ALU.is_ge).then_inc(big_ready, 1)
            dve.wait_ge(big_ready, 1)
            big = dve.value_load(bign[0:1, 0:1], min_val=0, max_val=1)
            dve.wait_ge(adj_self, T)
            weigh_turned(1)
            first_h(0)
            with dve.If(big < 1):
                for s in range(T):
                    dve.tensor_copy(adj_r[:, s, 0:N], adj[:, 0, s, 0:N])
            dve.memset(rs0[:], 0.0).then_inc(adj_exact, 1)
            with dve.Fori(1, T // 2 - 1) as c:
                weigh_turned(c + 1)
                first_h(c)
            first_h(T // 2 - 1)
            dve.wait_ge(rows_in, 48)

            def row(a, i):
                return a[:, bass.ds(i, 1)].rearrange("p o d -> p (o d)")

            def layer(i):
                dve.wait_ge(z_mm, i + 1)
                for c, (c0, n) in enumerate(CH):
                    dve.tensor_copy(zT[:, 1, c0:c0 + n], pb[:, 3 + c, 0:n]).then_inc(z_hi, 1)
                for c, (c0, n) in enumerate(CH):
                    dve.wait_ge(wa_mm, i * 6 + 2 * c + 2)
                    dve.tensor_scalar(rT[:, 1, c0:c0 + n], pb[:, 3 + c, 0:n],
                                      ba_c[:, 1:2], 0.0,
                                      ALU.add, ALU.max).then_inc(r_hi, 1)

                def stats(t):
                    v = i * T + t + 1
                    dve.wait_ge(wb_mm, v)
                    dve.tensor_tensor(zt[:, t % 2], pb[0:P, 6 + t % 2, 0:HB], row(bb_b, i), ALU.add).then_inc(z_b, 1)
                    dve.wait_ge(z_b, 1 + v)
                    dve.bn_stats(st4[:, t % 2], zt[:, t % 2]).then_inc(z_stats, 1)
                    wait_apart(dve, z_stats, v)
                    dve.bn_aggr(mv4[:, t % 2], st4[:, t % 2]).then_inc(z_mv, 1)

                def update(t):
                    v = i * T + t + 1
                    dve.wait_ge(z_mv, v)
                    dve.scalar_tensor_tensor(zt[:, 2 + 2 * (t % 2)], zt[:, t % 2], mv4[:, t % 2, 0:1], row(ng_b, i),
                                             ALU.subtract, ALU.mult).then_inc(z_gain, 1)
                    dve.wait_ge(z_sd, v)
                    dve.reciprocal(small4[:, t % 2:t % 2 + 1], small4[:, 2 + t % 2:3 + t % 2]).then_inc(z_rstd, 1)
                    dve.wait_ge(z_rstd, v)
                    dve.wait_ge(z_gain, v)
                    dve.scalar_tensor_tensor(zt[:, 3], zt[:, 2 + 2 * (t % 2)], small4[:, t % 2:t % 2 + 1], row(nb_b, i),
                                             ALU.mult, ALU.add).then_inc(z_bias, 1)
                    dve.wait_ge(z_bias, v)
                    dve.scalar_tensor_tensor(h[:, t], zt[:, 3], 0.0, h[:, t], ALU.max, ALU.add).then_inc(h_done, 1)

                stats(0)
                for t in range(T):
                    if t + 1 < T:
                        stats(t + 1)
                    update(t)

            with dve.Fori(0, L) as i:
                layer(i)

            def stats_of(c, s_stats, m, s_mv):
                for u in range(2):
                    dve.bn_stats(st5[:, u, 0], s5[:, u, 0:512])
                    dve.bn_stats(st5[:, u, 1], s5[:, u, 512:D]).then_inc(s_stats, 1)
                wait_apart(dve, s_stats, c * 2 + 2)
                for u in range(2):
                    ins = dve.bn_aggr(m[:, u], st5[:, u].rearrange("p a b -> p (a b)"))
                ins.then_inc(s_mv, 1)

            with dve.Fori(0, T // 2) as c:
                dve.wait_ge(xb_done, c + 1)
                dve.wait_ge(f_done, 1 + c * 2)
                for u in range(2):
                    dve.wait_ge(d2_mm, 1 + c * 2 + u + 1)
                    dve.tensor_tensor(s5[:, u], pb[0:P, 3 + 2 * u:5 + 2 * u].rearrange("p a b -> p (a b)"),
                                      x_bd[:, u], ALU.add).then_inc(o_sum, 1)
                dve.wait_ge(o_sum, 1 + c * 2 + 2)
                stats_of(c, o_stats, mv4, o_mv)
                dve.wait_ge(o_mv, c + 1)
                for u in range(2):
                    dve.scalar_tensor_tensor(s5[:, u], s5[:, u], mv4[:, u, 0:1], go_b[:], ALU.subtract,
                                             ALU.mult).then_inc(o_gain, 1)
                dve.wait_ge(o_sd, c + 1)
                dve.reciprocal(rs5[:, 0], sd5[:, 0]).then_inc(o_rstd, 1)
                dve.wait_ge(o_rstd, c + 1)
                dve.wait_ge(xo_done, c + 1)
                dve.wait_ge(o_gain, c * 2 + 2)
                for u in range(2):
                    ins = dve.scalar_tensor_tensor(s5[:, u], s5[:, u], rs5[:, 0, u:u + 1], x_bo[:, u], ALU.mult,
                                                   ALU.add)
                ins.then_inc(o_res, 1)
                dve.wait_ge(o_res, 1 + c + 1)
                stats_of(c, f_stats, mv5, f_mv)
                dve.wait_ge(f_sd, c + 1)
                dve.reciprocal(rs5[:, 1], sd5[:, 1]).then_inc(f_rstd, 1)
                dve.wait_ge(f_rstd, c + 1)
                for u in range(2):
                    dve.wait_ge(out_done, 16 + (c * 2) * 16)
                    dve.tensor_scalar(ot[:, u], s5[:, u], mv5[:, u, 0:1], rs5[:, 1, u:u + 1], ALU.subtract,
                                      ALU.mult).then_inc(f_done, 1)


_INS = ['x', 'src', 'dst', 'edge_type_2', 'L0_gnn_ln_weight', 'L0_gnn_W_rel', 'L0_gnn_W_root',
        'L0_gnn_conv_bias', 'L0_gnn_wo_weight', 'L1_gnn_ln_in_g', 'L1_gnn_ln_in_b', 'L1_gnn_W1',
        'L1_gnn_b1', 'L1_gnn_W2', 'L1_gnn_b2', 'L1_gnn_layer_Wa', 'L1_gnn_layer_ba',
        'L1_gnn_layer_Wb', 'L1_gnn_layer_bb', 'L1_gnn_layer_ng', 'L1_gnn_layer_nb', 'L1_gnn_Wd1',
        'L1_gnn_bd1', 'L1_gnn_Wd2', 'L1_gnn_bd2', 'L1_gnn_out_g', 'L1_gnn_out_b']


def kernel(**inputs):
    import numpy as _np
    import concourse.bacc as _bacc
    from concourse import mybir as _mybir
    from concourse.bass_utils import run_bass_kernel_spmd as _run

    nc = _bacc.Bacc("TRN2", target_bir_lowering=False, num_devices=1)
    arrays, args = {}, []
    for name in _INS:
        a = _np.ascontiguousarray(inputs[name])
        arrays[f"in_{name}"] = a
        args.append(nc.dram_tensor(f"in_{name}", a.shape, _mybir.dt.from_np(a.dtype), kind="ExternalInput").ap())
    out = nc.dram_tensor("out_x", (N, D), F32, kind="ExternalOutput").ap()
    graph_kernel(nc, *args, out)
    r = _run(nc, [arrays], core_ids=[0])
    return r.results[0]["out_x"]
```
